# Optimizing a Trainium2 kernel written in Bass

```python
import numpy as np
import jax
import jax.numpy as jnp

def _softmax(x, axis=-1):
    return jax.nn.softmax(x, axis=axis)

def _gelu(x):
    return jax.nn.gelu(x, approximate=True)

def _silu(x):
    return jax.nn.silu(x)

def _sigmoid(x):
    return jax.nn.sigmoid(x)

def _layernorm(x, axis=-1, eps=1e-05):
    m = jnp.mean(x, axis=axis, keepdims=True)
    v = jnp.var(x, axis=axis, keepdims=True)
    return (x - m) / jnp.sqrt(v + eps)

def _scatter_add(tgt, idx, src, axis=0):
    return tgt.at[idx].add(src)

def _segment_sum(src, seg, n):
    return jax.ops.segment_sum(src, seg, n)
kernel_name = 'mk_perceiver_d2_seqx_r8_26a1c9'

def setup_inputs(seed: int=0):
    np.random.seed(seed)
    _w = jnp.asarray

    def _rec_inputs():
        import jax
        import jax.numpy as jnp
        _rk = jax.random.key(seed)
        x = -0.0001661 + 0.9999 * jax.random.normal(jax.random.fold_in(_rk, 1), (8, 64, 256), jnp.float32)
        _lenS = 64 - jax.random.randint(jax.random.fold_in(_rk, 7), (8,), 0, max(1, 64 // 4) + 1, jnp.int32)
        _lenS2 = 1601 - jax.random.randint(jax.random.fold_in(_rk, 8), (8,), 0, max(1, 1601 // 4) + 1, jnp.int32)
        _ctx_2048P = jax.random.normal(jax.random.fold_in(_rk, 11), (8, 16, 256), jnp.float32)
        _ctx_2048c = jax.random.dirichlet(jax.random.fold_in(_rk, 511), 0.3 * jnp.ones((16,), jnp.float32), (8, 1601))
        _ctx_2048t = jnp.einsum('bsk,bkd->bsd', _ctx_2048c, _ctx_2048P)
        _ctx_2048t = _ctx_2048t * jax.lax.rsqrt(jnp.mean(jnp.square(_ctx_2048t)) + 1e-12) * 0.953939
        ctx_2048 = -0.00016346 + 1.00032 * (_ctx_2048t + 0.3 * jax.random.normal(jax.random.fold_in(_rk, 611), (8, 1601, 256), jnp.float32))
        pos_BxS2 = jnp.broadcast_to(jnp.arange(1601, dtype=jnp.int32), (8, 1601))
        itok_BxS_4096_4607 = jax.random.randint(jax.random.fold_in(_rk, 14), (8, 64), 512, 576, jnp.int32)
        return (x, ctx_2048, pos_BxS2, itok_BxS_4096_4607, _lenS2)
    x, ctx_2048, pos_BxS2, itok_BxS_4096_4607, _lenS2 = _rec_inputs()

    def _L0_xattn_setup():
        import jax, jax.numpy as jnp
        import numpy as np
        DIM = 256
        HEADS = 16
        HEAD_DIM = DIM // HEADS
        EPS = 1e-06
        IMG_TOKENS = 257
        B, L1, L2 = (2, 512, 769)
        SCALE = 1.0 / np.sqrt(HEAD_DIM).astype(np.float32)

        def rms_norm(x, g):
            return x * jax.lax.rsqrt(jnp.mean(x * x, axis=-1, keepdims=True) + EPS) * g

        def attention(q, k, v, kv_mask=None):
            s = jnp.einsum('bqhd,bkhd->bhqk', q, k) * SCALE
            if kv_mask is not None:
                s = jnp.where(kv_mask[:, None, None, :], s, jnp.float32(-1000000000.0))
            p = jax.nn.softmax(s, axis=-1)
            return jnp.einsum('bhqk,bkhd->bqhd', p, v)
        key = jax.random.key(seed)
        ks = jax.random.split(key, 20)
        std = 0.02

        def lin(i):
            return (jax.random.normal(ks[i], (DIM, DIM), jnp.float32) * std, jnp.zeros((DIM,), jnp.float32))
        w_q, b_q = lin(0)
        w_k, b_k = lin(1)
        w_v, b_v = lin(2)
        w_k_img, b_k_img = lin(3)
        w_v_img, b_v_img = lin(4)
        w_o, b_o = lin(5)
        return {'x': jax.random.normal(ks[6], (B, L1, DIM), jnp.float32), 'context': jax.random.normal(ks[7], (B, L2, DIM), jnp.float32), 'context_lens': jax.random.randint(ks[8], (B,), 32, 513, jnp.int64 if jax.config.jax_enable_x64 else jnp.int32), 'w_q': w_q, 'b_q': b_q, 'w_k': w_k, 'b_k': b_k, 'w_v': w_v, 'b_v': b_v, 'w_k_img': w_k_img, 'b_k_img': b_k_img, 'w_v_img': w_v_img, 'b_v_img': b_v_img, 'w_o': w_o, 'b_o': b_o, 'g_q': jnp.ones((DIM,), jnp.float32), 'g_k': jnp.ones((DIM,), jnp.float32), 'g_k_img': jnp.ones((DIM,), jnp.float32)}
    _L0_xattn_all = _L0_xattn_setup()
    _L0_xattn_in = {k: v for k, v in _L0_xattn_all.items() if k in ('w_q', 'b_q', 'w_k', 'b_k', 'w_v', 'b_v', 'w_k_img', 'b_k_img', 'w_v_img', 'b_v_img', 'w_o', 'b_o', 'g_q', 'g_k', 'g_k_img')}
    del _L0_xattn_all

    def _L0_attn_setup():
        import math
        import jax, jax.numpy as jnp
        import numpy as np
        H, KV, D = (16, 4, 128)
        HID = 256
        ROPE_BASE = 1000000.0
        EPS = 1e-06

        def _layernorm(x, w, b):
            mu = jnp.mean(x, axis=-1, keepdims=True)
            xc = x - mu
            var = jnp.mean(xc * xc, axis=-1, keepdims=True)
            return xc * jax.lax.rsqrt(var + EPS) * w + b

        def _rope(x, cos, sin):
            xr, xi = (x[..., 0::2], x[..., 1::2])
            c, s = (cos[None, None], sin[None, None])
            out = jnp.stack([xr * c - xi * s, xr * s + xi * c], axis=-1)
            return out.reshape(x.shape)
        key = jax.random.key(seed)
        ks = jax.random.split(key, 3)
        B, S = (2, 256)
        s = 0.02
        return {'x': jax.random.normal(ks[0], (B, S, HID), jnp.float32), 'w_qkv': jax.random.normal(ks[1], (2 * H * D + 2 * KV * D, HID), jnp.float32) * s, 'w_o': jax.random.normal(ks[2], (HID, H * D), jnp.float32) * s, 'q_norm_w': jnp.ones((D,), jnp.float32), 'q_norm_b': jnp.zeros((D,), jnp.float32), 'k_norm_w': jnp.ones((D,), jnp.float32), 'k_norm_b': jnp.zeros((D,), jnp.float32)}
    _L0_attn_all = _L0_attn_setup()
    _L0_attn_in = {k: v for k, v in _L0_attn_all.items() if k in ('w_qkv', 'w_o', 'q_norm_w', 'q_norm_b', 'k_norm_w', 'k_norm_b')}
    del _L0_attn_all

    def _L0_ffn_setup():
        import jax, jax.numpy as jnp
        import numpy as np
        N, S, D = (8, 256, 256)
        O = 256
        E = 8
        K = 2
        key = jax.random.key(seed)
        ks = jax.random.split(key, 5)
        scale_in = 1.0 / np.sqrt(D)
        x = jax.random.normal(ks[0], (N, S, D), dtype=jnp.float32)
        gate_w = jax.random.uniform(ks[1], (D, E), dtype=jnp.float32, minval=-scale_in, maxval=scale_in)
        gate_b = jax.random.uniform(ks[2], (E,), dtype=jnp.float32, minval=-scale_in, maxval=scale_in)
        expert_w = jax.random.uniform(ks[3], (E, D, O), dtype=jnp.float32, minval=-scale_in, maxval=scale_in)
        expert_b = jax.random.uniform(ks[4], (E, O), dtype=jnp.float32, minval=-scale_in, maxval=scale_in)
        return {'x': x, 'gate_w': gate_w, 'gate_b': gate_b, 'expert_w': expert_w, 'expert_b': expert_b}
    _L0_ffn_all = _L0_ffn_setup()
    _L0_ffn_in = {k: v for k, v in _L0_ffn_all.items() if k in ('gate_w', 'gate_b', 'expert_w', 'expert_b')}
    del _L0_ffn_all

    def _L1_xattn_setup():
        import jax, jax.numpy as jnp
        import numpy as np
        B, CTX, DRAFT, D = (2, 512, 64, 256)
        H, KVH, HD = (16, 4, 128)
        N_REP = H // KVH
        EPS = 1e-06
        THETA = 10000.0
        SCALE = 1.0 / np.sqrt(HD).astype(np.float32)

        def _rms_norm(x, w):
            v = jnp.mean(jnp.square(x.astype(jnp.float32)), axis=-1, keepdims=True)
            return (w * (x.astype(jnp.float32) * jax.lax.rsqrt(v + EPS))).astype(x.dtype)

        def _rotate_half(x):
            x1, x2 = jnp.split(x, 2, axis=-1)
            return jnp.concatenate((-x2, x1), axis=-1)

        def _rope(x, pos):
            inv_freq = 1.0 / THETA ** (jnp.arange(0, HD, 2, dtype=jnp.float32) / HD)
            freqs = pos.astype(jnp.float32)[:, None, :, None] * inv_freq
            emb = jnp.concatenate((freqs, freqs), axis=-1)
            return x * jnp.cos(emb) + _rotate_half(x) * jnp.sin(emb)
        key = jax.random.key(seed)
        ks = jax.random.split(key, 6)
        return {'draft_hidden': jax.random.normal(ks[0], (B, DRAFT, D), jnp.float32), 'context_hidden': jax.random.normal(ks[1], (B, CTX, D), jnp.float32), 'Wq': jax.random.normal(ks[2], (H * HD, D), jnp.float32) * 0.02, 'Wk': jax.random.normal(ks[3], (KVH * HD, D), jnp.float32) * 0.02, 'Wv': jax.random.normal(ks[4], (KVH * HD, D), jnp.float32) * 0.02, 'Wo': jax.random.normal(ks[5], (D, H * HD), jnp.float32) * 0.02, 'q_norm_w': jnp.ones((HD,), jnp.float32), 'k_norm_w': jnp.ones((HD,), jnp.float32), 'context_position_ids': jnp.broadcast_to(jnp.arange(CTX, dtype=jnp.int32), (B, CTX)), 'draft_position_ids': jnp.broadcast_to(CTX + jnp.arange(DRAFT, dtype=jnp.int32), (B, DRAFT))}
    _L1_xattn_all = _L1_xattn_setup()
    _L1_xattn_in = {k: v for k, v in _L1_xattn_all.items() if k in ('Wq', 'Wk', 'Wv', 'Wo', 'q_norm_w', 'k_norm_w')}
    del _L1_xattn_all

    def _L1_attn_setup():
        import jax, jax.numpy as jnp
        import numpy as np
        HEAD = 16
        THETA = 30000.0

        def _layernorm(x, g, b, eps=1e-05):
            mu = jnp.mean(x, axis=-1, keepdims=True)
            var = jnp.mean((x - mu) ** 2, axis=-1, keepdims=True)
            return (x - mu) * jax.lax.rsqrt(var + eps) * g + b

        def _rotary(t, xa):
            B, H, C, D = t.shape
            pos = jnp.arange(C, dtype=t.dtype)
            freqs = jnp.arange(0, D, 2, dtype=t.dtype) / D * jnp.log(jnp.asarray(THETA, t.dtype))
            ang = pos[:, None] * freqs[None, :]
            m = jnp.linalg.norm(xa, axis=-1, keepdims=True)
            fre = (m * jnp.cos(ang))[:, None]
            fim = (m * jnp.sin(ang))[:, None]
            tp = t.reshape(B, H, C, D // 2, 2)
            a, b = (tp[..., 0], tp[..., 1])
            out = jnp.stack([a * fre - b * fim, a * fim + b * fre], axis=-1)
            return out.reshape(B, H, C, D)
        key = jax.random.key(seed)
        ks = jax.random.split(key, 4)
        B, C, Dm = (1, 256, 256)
        hd = Dm // HEAD
        w = 0.02
        return {'x': jax.random.normal(ks[0], (B, C, Dm), jnp.float32), 'qn_g': jnp.ones((Dm,), jnp.float32), 'qn_b': jnp.zeros((Dm,), jnp.float32), 'kvn_g': jnp.ones((Dm,), jnp.float32), 'kvn_b': jnp.zeros((Dm,), jnp.float32), 'Wq': w * jax.random.normal(ks[1], (Dm, Dm), jnp.float32), 'bq': jnp.zeros((Dm,), jnp.float32), 'Wkv': w * jax.random.normal(ks[2], (Dm, 2 * Dm), jnp.float32), 'bkv': jnp.zeros((2 * Dm,), jnp.float32), 'Wo': w * jax.random.normal(ks[3], (Dm, Dm), jnp.float32), 'bo': jnp.zeros((Dm,), jnp.float32), 'ln_g': jnp.ones((hd,), jnp.float32), 'ln_b': jnp.zeros((hd,), jnp.float32)}
    _L1_attn_all = _L1_attn_setup()
    _L1_attn_in = {k: v for k, v in _L1_attn_all.items() if k in ('qn_g', 'qn_b', 'kvn_g', 'kvn_b', 'Wq', 'bq', 'Wkv', 'bkv', 'Wo', 'bo', 'ln_g', 'ln_b')}
    del _L1_attn_all

    def _L1_ffn_setup():
        import jax, jax.numpy as jnp
        import numpy as np
        NUM_EXPERTS = 8
        TOP_K = 2
        IN_DIM = 256
        BOT_DIM = 64
        BATCH, SEQ = (4, 256)

        def _gelu(x):
            return jax.nn.gelu(x, approximate=False)
        key = jax.random.key(seed)
        ks = jax.random.split(key, 8)
        scale_d = 1.0 / np.sqrt(IN_DIM)
        scale_b = 1.0 / np.sqrt(BOT_DIM)
        return {'hidden_states': jax.random.normal(ks[0], (BATCH, SEQ, IN_DIM), jnp.float32), 'gate_w': jax.random.normal(ks[1], (NUM_EXPERTS, IN_DIM), jnp.float32) * scale_d, 'wd': jax.random.normal(ks[2], (NUM_EXPERTS, BOT_DIM, IN_DIM), jnp.float32) * scale_d, 'bd': jnp.zeros((NUM_EXPERTS, BOT_DIM), jnp.float32), 'wu': jax.random.normal(ks[3], (NUM_EXPERTS, IN_DIM, BOT_DIM), jnp.float32) * scale_b * 0.02, 'bu': jnp.zeros((NUM_EXPERTS, IN_DIM), jnp.float32), 'ws_d': jax.random.normal(ks[4], (BOT_DIM, IN_DIM), jnp.float32) * scale_d, 'bs_d': jnp.zeros((BOT_DIM,), jnp.float32), 'ws_u': jax.random.normal(ks[5], (IN_DIM, BOT_DIM), jnp.float32) * scale_b * 0.02, 'bs_u': jnp.zeros((IN_DIM,), jnp.float32)}
    _L1_ffn_all = _L1_ffn_setup()
    _L1_ffn_in = {k: v for k, v in _L1_ffn_all.items() if k in ('gate_w', 'wd', 'bd', 'wu', 'bu', 'ws_d', 'bs_d', 'ws_u', 'bs_u')}
    del _L1_ffn_all
    return {'x': x, 'ctx_2048': ctx_2048, 'pos_BxS2': pos_BxS2, 'itok_BxS_4096_4607': itok_BxS_4096_4607, '_lenS2': _lenS2, 'L0_xattn_w_q': _L0_xattn_in['w_q'], 'L0_xattn_b_q': _L0_xattn_in['b_q'], 'L0_xattn_w_k': _L0_xattn_in['w_k'], 'L0_xattn_b_k': _L0_xattn_in['b_k'], 'L0_xattn_w_v': _L0_xattn_in['w_v'], 'L0_xattn_b_v': _L0_xattn_in['b_v'], 'L0_xattn_w_k_img': _L0_xattn_in['w_k_img'], 'L0_xattn_b_k_img': _L0_xattn_in['b_k_img'], 'L0_xattn_w_v_img': _L0_xattn_in['w_v_img'], 'L0_xattn_b_v_img': _L0_xattn_in['b_v_img'], 'L0_xattn_w_o': _L0_xattn_in['w_o'], 'L0_xattn_b_o': _L0_xattn_in['b_o'], 'L0_xattn_g_q': _L0_xattn_in['g_q'], 'L0_xattn_g_k': _L0_xattn_in['g_k'], 'L0_xattn_g_k_img': _L0_xattn_in['g_k_img'], 'L0_attn_w_qkv': _L0_attn_in['w_qkv'], 'L0_attn_w_o': _L0_attn_in['w_o'], 'L0_attn_q_norm_w': _L0_attn_in['q_norm_w'], 'L0_attn_q_norm_b': _L0_attn_in['q_norm_b'], 'L0_attn_k_norm_w': _L0_attn_in['k_norm_w'], 'L0_attn_k_norm_b': _L0_attn_in['k_norm_b'], 'L0_ffn_gate_w': _L0_ffn_in['gate_w'], 'L0_ffn_gate_b': _L0_ffn_in['gate_b'], 'L0_ffn_expert_w': _L0_ffn_in['expert_w'], 'L0_ffn_expert_b': _L0_ffn_in['expert_b'], 'L1_xattn_Wq': _L1_xattn_in['Wq'], 'L1_xattn_Wk': _L1_xattn_in['Wk'], 'L1_xattn_Wv': _L1_xattn_in['Wv'], 'L1_xattn_Wo': _L1_xattn_in['Wo'], 'L1_xattn_q_norm_w': _L1_xattn_in['q_norm_w'], 'L1_xattn_k_norm_w': _L1_xattn_in['k_norm_w'], 'L1_attn_qn_g': _L1_attn_in['qn_g'], 'L1_attn_qn_b': _L1_attn_in['qn_b'], 'L1_attn_kvn_g': _L1_attn_in['kvn_g'], 'L1_attn_kvn_b': _L1_attn_in['kvn_b'], 'L1_attn_Wq': _L1_attn_in['Wq'], 'L1_attn_bq': _L1_attn_in['bq'], 'L1_attn_Wkv': _L1_attn_in['Wkv'], 'L1_attn_bkv': _L1_attn_in['bkv'], 'L1_attn_Wo': _L1_attn_in['Wo'], 'L1_attn_bo': _L1_attn_in['bo'], 'L1_attn_ln_g': _L1_attn_in['ln_g'], 'L1_attn_ln_b': _L1_attn_in['ln_b'], 'L1_ffn_gate_w': _L1_ffn_in['gate_w'], 'L1_ffn_wd': _L1_ffn_in['wd'], 'L1_ffn_bd': _L1_ffn_in['bd'], 'L1_ffn_wu': _L1_ffn_in['wu'], 'L1_ffn_bu': _L1_ffn_in['bu'], 'L1_ffn_ws_d': _L1_ffn_in['ws_d'], 'L1_ffn_bs_d': _L1_ffn_in['bs_d'], 'L1_ffn_ws_u': _L1_ffn_in['ws_u'], 'L1_ffn_bs_u': _L1_ffn_in['bs_u']}

def reference(x, ctx_2048, pos_BxS2, itok_BxS_4096_4607, _lenS2, L0_xattn_w_q, L0_xattn_b_q, L0_xattn_w_k, L0_xattn_b_k, L0_xattn_w_v, L0_xattn_b_v, L0_xattn_w_k_img, L0_xattn_b_k_img, L0_xattn_w_v_img, L0_xattn_b_v_img, L0_xattn_w_o, L0_xattn_b_o, L0_xattn_g_q, L0_xattn_g_k, L0_xattn_g_k_img, L0_attn_w_qkv, L0_attn_w_o, L0_attn_q_norm_w, L0_attn_q_norm_b, L0_attn_k_norm_w, L0_attn_k_norm_b, L0_ffn_gate_w, L0_ffn_gate_b, L0_ffn_expert_w, L0_ffn_expert_b, L1_xattn_Wq, L1_xattn_Wk, L1_xattn_Wv, L1_xattn_Wo, L1_xattn_q_norm_w, L1_xattn_k_norm_w, L1_attn_qn_g, L1_attn_qn_b, L1_attn_kvn_g, L1_attn_kvn_b, L1_attn_Wq, L1_attn_bq, L1_attn_Wkv, L1_attn_bkv, L1_attn_Wo, L1_attn_bo, L1_attn_ln_g, L1_attn_ln_b, L1_ffn_gate_w, L1_ffn_wd, L1_ffn_bd, L1_ffn_wu, L1_ffn_bu, L1_ffn_ws_d, L1_ffn_bs_d, L1_ffn_ws_u, L1_ffn_bs_u):
    import jax
    import jax.numpy as jnp

    def _L0_xattn_ref(x, context, context_lens, w_q, b_q, w_k, b_k, w_v, b_v, w_k_img, b_k_img, w_v_img, b_v_img, w_o, b_o, g_q, g_k, g_k_img):
        import jax, jax.numpy as jnp
        import numpy as np
        DIM = 256
        HEADS = 16
        HEAD_DIM = DIM // HEADS
        EPS = 1e-06
        IMG_TOKENS = 257
        B, L1, L2 = (2, 512, 769)
        SCALE = 1.0 / np.sqrt(HEAD_DIM).astype(np.float32)

        def rms_norm(x, g):
            return x * jax.lax.rsqrt(jnp.mean(x * x, axis=-1, keepdims=True) + EPS) * g

        def attention(q, k, v, kv_mask=None):
            s = jnp.einsum('bqhd,bkhd->bhqk', q, k) * SCALE
            if kv_mask is not None:
                s = jnp.where(kv_mask[:, None, None, :], s, jnp.float32(-1000000000.0))
            p = jax.nn.softmax(s, axis=-1)
            return jnp.einsum('bhqk,bkhd->bqhd', p, v)
        b = x.shape[0]
        ctx_img = context[:, :IMG_TOKENS]
        ctx_txt = context[:, IMG_TOKENS:]
        q = rms_norm(x @ w_q.T + b_q, g_q).reshape(b, -1, HEADS, HEAD_DIM)
        k = rms_norm(ctx_txt @ w_k.T + b_k, g_k).reshape(b, -1, HEADS, HEAD_DIM)
        v = (ctx_txt @ w_v.T + b_v).reshape(b, -1, HEADS, HEAD_DIM)
        k_img = rms_norm(ctx_img @ w_k_img.T + b_k_img, g_k_img).reshape(b, -1, HEADS, HEAD_DIM)
        v_img = (ctx_img @ w_v_img.T + b_v_img).reshape(b, -1, HEADS, HEAD_DIM)
        txt_len = ctx_txt.shape[1]
        kv_mask = jnp.arange(txt_len)[None, :] < context_lens[:, None]
        img_x = attention(q, k_img, v_img)
        txt_x = attention(q, k, v, kv_mask)
        out = (txt_x + img_x).reshape(b, -1, DIM)
        return out @ w_o.T + b_o

    def _L0_attn_ref(x, w_qkv, w_o, q_norm_w, q_norm_b, k_norm_w, k_norm_b):
        import math
        import jax, jax.numpy as jnp
        import numpy as np
        H, KV, D = (16, 4, 128)
        HID = 256
        ROPE_BASE = 1000000.0
        EPS = 1e-06

        def _layernorm(x, w, b):
            mu = jnp.mean(x, axis=-1, keepdims=True)
            xc = x - mu
            var = jnp.mean(xc * xc, axis=-1, keepdims=True)
            return xc * jax.lax.rsqrt(var + EPS) * w + b

        def _rope(x, cos, sin):
            xr, xi = (x[..., 0::2], x[..., 1::2])
            c, s = (cos[None, None], sin[None, None])
            out = jnp.stack([xr * c - xi * s, xr * s + xi * c], axis=-1)
            return out.reshape(x.shape)
        B, S, _ = x.shape
        qkv = x @ w_qkv.T
        qg, k, v = jnp.split(qkv, [2 * H * D, 2 * H * D + KV * D], axis=-1)
        q, gate = jnp.split(qg, 2, axis=-1)
        q = q.reshape(B, S, H, D).transpose(0, 2, 1, 3)
        k = k.reshape(B, S, KV, D).transpose(0, 2, 1, 3)
        v = v.reshape(B, S, KV, D).transpose(0, 2, 1, 3)
        q = _layernorm(q, q_norm_w, q_norm_b)
        k = _layernorm(k, k_norm_w, k_norm_b)
        inv = 1.0 / ROPE_BASE ** (jnp.arange(0, D, 2, dtype=jnp.float32) / D)
        freqs = jnp.outer(jnp.arange(S, dtype=jnp.float32), inv)
        cos, sin = (jnp.cos(freqs), jnp.sin(freqs))
        q = _rope(q, cos, sin)
        k = _rope(k, cos, sin)
        rep = H // KV
        k = jnp.repeat(k, rep, axis=1)
        v = jnp.repeat(v, rep, axis=1)
        scores = jnp.einsum('bhqd,bhkd->bhqk', q, k) / math.sqrt(D)
        causal = jnp.tril(jnp.ones((S, S), bool))
        scores = jnp.where(causal[None, None], scores, -jnp.inf)
        attn = jax.nn.softmax(scores, axis=-1)
        out = jnp.einsum('bhqk,bhkd->bhqd', attn, v)
        out = out.transpose(0, 2, 1, 3).reshape(B, S, H * D)
        out = out * jax.nn.sigmoid(gate)
        return out @ w_o.T

    def _L0_ffn_ref(x, gate_w, gate_b, expert_w, expert_b):
        import jax, jax.numpy as jnp
        import numpy as np
        N, S, D = (8, 256, 256)
        O = 256
        E = 8
        K = 2
        gate_logits = jnp.einsum('nsd,de->nse', x, gate_w) + gate_b
        _, top_idx = jax.lax.top_k(gate_logits, K)
        all_out = jax.nn.relu(jnp.einsum('nsd,edo->nseo', x, expert_w) + expert_b)
        sel = jnp.take_along_axis(all_out, top_idx[..., None], axis=2)
        return sel.mean(axis=2)

    def _L1_xattn_ref(draft_hidden, context_hidden, Wq, Wk, Wv, Wo, q_norm_w, k_norm_w, context_position_ids, draft_position_ids):
        import jax, jax.numpy as jnp
        import numpy as np
        B, CTX, DRAFT, D = (2, 512, 64, 256)
        H, KVH, HD = (16, 4, 128)
        N_REP = H // KVH
        EPS = 1e-06
        THETA = 10000.0
        SCALE = 1.0 / np.sqrt(HD).astype(np.float32)

        def _rms_norm(x, w):
            v = jnp.mean(jnp.square(x.astype(jnp.float32)), axis=-1, keepdims=True)
            return (w * (x.astype(jnp.float32) * jax.lax.rsqrt(v + EPS))).astype(x.dtype)

        def _rotate_half(x):
            x1, x2 = jnp.split(x, 2, axis=-1)
            return jnp.concatenate((-x2, x1), axis=-1)

        def _rope(x, pos):
            inv_freq = 1.0 / THETA ** (jnp.arange(0, HD, 2, dtype=jnp.float32) / HD)
            freqs = pos.astype(jnp.float32)[:, None, :, None] * inv_freq
            emb = jnp.concatenate((freqs, freqs), axis=-1)
            return x * jnp.cos(emb) + _rotate_half(x) * jnp.sin(emb)
        bsz, draft_len, _ = draft_hidden.shape
        ctx_len = context_hidden.shape[1]
        total_len = ctx_len + draft_len
        q = (draft_hidden @ Wq.T).reshape(bsz, draft_len, H, HD)
        q = _rms_norm(q, q_norm_w).transpose(0, 2, 1, 3)
        kv_in = jnp.concatenate([context_hidden, draft_hidden], axis=1)
        k = (kv_in @ Wk.T).reshape(bsz, total_len, KVH, HD)
        v = (kv_in @ Wv.T).reshape(bsz, total_len, KVH, HD).transpose(0, 2, 1, 3)
        k = _rms_norm(k, k_norm_w).transpose(0, 2, 1, 3)
        full_position_ids = jnp.concatenate([context_position_ids, draft_position_ids], axis=1)
        q = _rope(q, draft_position_ids)
        k = _rope(k, full_position_ids)
        k = jnp.repeat(k, N_REP, axis=1)
        v = jnp.repeat(v, N_REP, axis=1)
        scores = jnp.einsum('bhqd,bhkd->bhqk', q, k) * SCALE
        probs = jax.nn.softmax(scores, axis=-1)
        attn = jnp.einsum('bhqk,bhkd->bhqd', probs, v)
        attn = attn.transpose(0, 2, 1, 3).reshape(bsz, draft_len, H * HD)
        return attn @ Wo.T

    def _L1_attn_ref(x, qn_g, qn_b, kvn_g, kvn_b, Wq, bq, Wkv, bkv, Wo, bo, ln_g, ln_b):
        import jax, jax.numpy as jnp
        import numpy as np
        HEAD = 16
        THETA = 30000.0

        def _layernorm(x, g, b, eps=1e-05):
            mu = jnp.mean(x, axis=-1, keepdims=True)
            var = jnp.mean((x - mu) ** 2, axis=-1, keepdims=True)
            return (x - mu) * jax.lax.rsqrt(var + eps) * g + b

        def _rotary(t, xa):
            B, H, C, D = t.shape
            pos = jnp.arange(C, dtype=t.dtype)
            freqs = jnp.arange(0, D, 2, dtype=t.dtype) / D * jnp.log(jnp.asarray(THETA, t.dtype))
            ang = pos[:, None] * freqs[None, :]
            m = jnp.linalg.norm(xa, axis=-1, keepdims=True)
            fre = (m * jnp.cos(ang))[:, None]
            fim = (m * jnp.sin(ang))[:, None]
            tp = t.reshape(B, H, C, D // 2, 2)
            a, b = (tp[..., 0], tp[..., 1])
            out = jnp.stack([a * fre - b * fim, a * fim + b * fre], axis=-1)
            return out.reshape(B, H, C, D)
        B, C, Dm = x.shape
        H = HEAD
        hd = Dm // H
        scale = hd ** (-0.25)
        q = (_layernorm(x, qn_g, qn_b) @ Wq + bq).reshape(B, C, H, hd).transpose(0, 2, 1, 3)
        kv = (_layernorm(x, kvn_g, kvn_b) @ Wkv + bkv).reshape(B, C, 2, H, hd)
        kv = kv.transpose(2, 0, 3, 1, 4)
        k, v = (kv[0], kv[1])
        q = q * scale
        k = k * scale
        q = _rotary(q, x)
        k = _rotary(k, x)
        qn = _layernorm(q, ln_g, ln_b)
        kn = _layernorm(k, ln_g, ln_b)
        scores = jnp.einsum('bhqd,bhkd->bhqk', qn, kn) / jnp.sqrt(jnp.asarray(hd, x.dtype))
        causal = jnp.tril(jnp.ones((C, C), bool))
        scores = jnp.where(causal, scores, jnp.finfo(scores.dtype).min)
        w = jax.nn.softmax(scores, axis=-1)
        a = jnp.einsum('bhqk,bhkd->bhqd', w, v)
        out = a.transpose(0, 2, 1, 3).reshape(B, C, Dm) @ Wo + bo
        return out

    def _L1_ffn_ref(hidden_states, gate_w, wd, bd, wu, bu, ws_d, bs_d, ws_u, bs_u):
        import jax, jax.numpy as jnp
        import numpy as np
        NUM_EXPERTS = 8
        TOP_K = 2
        IN_DIM = 256
        BOT_DIM = 64
        BATCH, SEQ = (4, 256)

        def _gelu(x):
            return jax.nn.gelu(x, approximate=False)
        B, S, D = hidden_states.shape
        x = hidden_states.reshape(-1, D)
        T = x.shape[0]
        logits = x @ gate_w.T
        probs = jax.nn.softmax(logits.astype(jnp.float32), axis=-1)
        rw, sel = jax.lax.top_k(probs, TOP_K)
        rw = rw / rw.sum(axis=-1, keepdims=True)
        rw = rw.astype(x.dtype)
        combine = jnp.zeros((T, NUM_EXPERTS), x.dtype).at[jnp.arange(T)[:, None], sel].add(rw)
        down = jnp.einsum('td,ebd->teb', x, wd) + bd[None]
        h = _gelu(down) * combine[:, :, None]
        expert_out = jnp.einsum('teb,edb->td', h, wu) + combine @ bu
        shared = _gelu(x @ ws_d.T + bs_d) @ ws_u.T + bs_u
        out = (expert_out + shared).reshape(B, S, D)
        return out
    x = x + _L0_xattn_ref(_layernorm(x, axis=-1), ctx_2048, _lenS2, L0_xattn_w_q, L0_xattn_b_q, L0_xattn_w_k, L0_xattn_b_k, L0_xattn_w_v, L0_xattn_b_v, L0_xattn_w_k_img, L0_xattn_b_k_img, L0_xattn_w_v_img, L0_xattn_b_v_img, L0_xattn_w_o, L0_xattn_b_o, L0_xattn_g_q, L0_xattn_g_k, L0_xattn_g_k_img)
    x = x + _L0_attn_ref(_layernorm(x, axis=-1), L0_attn_w_qkv, L0_attn_w_o, L0_attn_q_norm_w, L0_attn_q_norm_b, L0_attn_k_norm_w, L0_attn_k_norm_b)
    x = x + _L0_ffn_ref(_layernorm(x, axis=-1), L0_ffn_gate_w, L0_ffn_gate_b, L0_ffn_expert_w, L0_ffn_expert_b)
    x = x + _L1_xattn_ref(_layernorm(x, axis=-1), ctx_2048, L1_xattn_Wq, L1_xattn_Wk, L1_xattn_Wv, L1_xattn_Wo, L1_xattn_q_norm_w, L1_xattn_k_norm_w, pos_BxS2, itok_BxS_4096_4607)
    x = x + _L1_attn_ref(_layernorm(x, axis=-1), L1_attn_qn_g, L1_attn_qn_b, L1_attn_kvn_g, L1_attn_kvn_b, L1_attn_Wq, L1_attn_bq, L1_attn_Wkv, L1_attn_bkv, L1_attn_Wo, L1_attn_bo, L1_attn_ln_g, L1_attn_ln_b)
    x = x + _L1_ffn_ref(_layernorm(x, axis=-1), L1_ffn_gate_w, L1_ffn_wd, L1_ffn_bd, L1_ffn_wu, L1_ffn_bu, L1_ffn_ws_d, L1_ffn_bs_d, L1_ffn_ws_u, L1_ffn_bs_u)
    return x

_drawn_inputs = setup_inputs


def setup_inputs(seed=0):
    import zlib

    import numpy as np

    out = dict(_drawn_inputs(seed))
    spreads = {'L0_xattn_b_q': (0.0, 0.309),
     'L0_xattn_b_k': (0.0, 0.8),
     'L0_xattn_b_v': (0.0, 0.1),
     'L0_xattn_b_k_img': (0.0, 0.8),
     'L0_xattn_b_v_img': (0.0, 0.1),
     'L0_xattn_b_o': (0.0, 0.1),
     'L0_xattn_g_q': (1.0, 0.6),
     'L0_xattn_g_k': (1.0, 0.6),
     'L0_xattn_g_k_img': (1.0, 0.6),
     'L0_attn_q_norm_w': (1.0, 0.6),
     'L0_attn_q_norm_b': (0.0, 0.8),
     'L0_attn_k_norm_w': (1.0, 0.6),
     'L0_attn_k_norm_b': (0.0, 0.561),
     'L1_xattn_q_norm_w': (1.0, 0.6),
     'L1_xattn_k_norm_w': (1.0, 0.6),
     'L1_attn_qn_g': (1.0, 0.6),
     'L1_attn_qn_b': (0.0, 0.8),
     'L1_attn_kvn_g': (1.0, 0.6),
     'L1_attn_kvn_b': (0.0, 0.719),
     'L1_attn_bq': (0.0, 0.8),
     'L1_attn_bkv': (0.0, 0.1),
     'L1_attn_bo': (0.0, 0.1),
     'L1_attn_ln_g': (1.0, 0.6),
     'L1_attn_ln_b': (0.0, 0.8),
     'L1_ffn_bd': (0.0, 0.8),
     'L1_ffn_bu': (0.0, 0.1),
     'L1_ffn_bs_d': (0.0, 0.8),
     'L1_ffn_bs_u': (0.0, 0.1)}
    factors = {'L0_ffn_expert_b': 3.253,
     'L1_ffn_wd': 7.041,
     'L1_ffn_wu': 6.408,
     'L1_ffn_ws_d': 5.085,
     'L1_ffn_ws_u': 4.61}
    for name, (base, spread) in spreads.items():
        noise = np.random.default_rng([zlib.crc32(name.encode()), seed]).standard_normal(out[name].shape)
        drawn = base * np.exp(spread * noise) if base else spread * noise
        out[name] = jnp.asarray(drawn.astype(out[name].dtype))
    for name, factor in factors.items():
        out[name] = (out[name] * factor).astype(out[name].dtype)
    return out
```

```python
from contextlib import ExitStack

import numpy as np

import concourse.bass as bass
from concourse import mybir

F32 = mybir.dt.float32
BF16 = mybir.dt.bfloat16
I32 = mybir.dt.int32
ALU = mybir.AluOpType
ACT = mybir.ActivationFunctionType
AX = mybir.AxisListType

BATCH, SEQ, DIM = 8, 64, 256
CTX = 1601
IMG = 257
TXT = CTX - IMG
P = 128
CH = DIM // P
TILES = BATCH * SEQ // P
NEG = -1.0e9


class Signal:

    def __init__(self, ctx, nc, name, per=1, unit=1, credit=0):
        self.sem = ctx.enter_context(nc.semaphore(name))
        self.per, self.unit, self.credit = per * unit, unit, credit

    def open(self, eng):
        eng.sem_inc(self.sem, self.credit)

    def at(self, t, k=1):
        return t * self.per + (k * self.unit + self.credit)

    def before(self, t):
        return t * self.per + self.credit


class Space:

    def __init__(self, nc, ctx, phase):
        self.nc, self.ctx, self.phase = nc, ctx, phase
        self.signals = []

    def sb(self, name, shape, dtype=F32):
        return self.ctx.enter_context(self.nc.sbuf_tensor(f"{self.phase}_{name}", shape, dtype))

    def ps(self, name, shape, dtype=F32):
        return self.ctx.enter_context(self.nc.psum_tensor(f"{self.phase}_{name}", shape, dtype))

    def sig(self, name, per=1, unit=1, credit=0):
        self.signals.append(Signal(self.ctx, self.nc, f"{self.phase}_{name}", per, unit, credit))
        return self.signals[-1]

    def dma(self, name, per=1, credit=0):
        return self.sig(name, per, 16, credit)

    def clear(self):
        with self.nc.Block() as block:
            @block.gpsimd
            def _(g):
                for signal in self.signals:
                    g.sem_clear(signal.sem)


class Norm:

    def __init__(self, S, rows, psum):
        self.rows, self.psum = rows, psum
        self.x = S.sb("x", [rows, DIM])
        self.stats = S.sb("ln_stats", [rows, 6])
        self.mean_var = S.sb("ln_mean_var", [rows, 2])
        self.log_var = S.sb("ln_log_var", [rows, 1])
        self.rstd = S.sb("ln_rstd", [rows, 1])
        self.xn = S.sb("xn", [rows, DIM])
        self.xnT = S.sb("xnT", [P, CH, rows])
        self.eps = S.sb("ln_eps", [P, 1])
        self.eps_set = S.sig("ln_eps_set")
        self.x_loaded = S.dma("x_loaded")
        self.paused = S.sig("ln_paused")
        self.stats_done = S.sig("ln_stats_done")
        self.mean_var_done = S.sig("ln_mean_var_done")
        self.log_done = S.sig("ln_log_done")
        self.rstd_done = S.sig("ln_rstd_done")
        self.xn_done = S.sig("xn_done")
        self.turned = S.sig("turned")
        self.xnT_done = S.sig("xnT_done")

    def setup_vector(self, v):
        v.memset(self.eps[:, :], 1e-5).then_inc(self.eps_set.sem, 1)

    def vector(self, v, t):
        v.wait_ge(self.x_loaded.sem, self.x_loaded.at(t))
        v.bn_stats(self.stats[:, :], self.x[:, :]).then_inc(self.stats_done.sem, 1)
        v.wait_ge(self.stats_done.sem, self.stats_done.at(t))
        v.sem_inc(self.paused.sem, 1)
        v.bn_aggr(self.mean_var[:, :], self.stats[:, :]).then_inc(self.mean_var_done.sem, 1)
        v.wait_ge(self.rstd_done.sem, self.rstd_done.at(t))
        v.tensor_scalar(self.xn[:, :], self.x[:, :], self.mean_var[:, 0:1], self.rstd[:, 0:1],
                                        ALU.subtract, ALU.mult).then_inc(self.xn_done.sem, 1)
        v.wait_ge(self.turned.sem, self.turned.at(t))
        v.tensor_copy(self.xnT[:, :, :], self.psum).then_inc(self.xnT_done.sem, 1)

    def scalar(self, a, t):
        a.wait_ge(self.mean_var_done.sem, self.mean_var_done.at(t))
        a.activation(self.log_var[:, :], self.mean_var[:, 1:2], ACT.Ln,
                                      bias=self.eps[0:self.rows, 0:1]).then_inc(self.log_done.sem, 1)
        a.wait_ge(self.log_done.sem, self.log_done.at(t))
        a.activation(self.rstd[:, :], self.log_var[:, :], ACT.Exp, scale=-0.5).then_inc(self.rstd_done.sem, 1)

    def tensor(self, pe, t, ident):
        pe.wait_ge(self.xn_done.sem, self.xn_done.at(t))
        if self.rows < P:
            pe.sem_inc(self.paused.sem, 1)
        for c in range(CH):
            turn = pe.transpose(self.psum[:, c, :], self.xn[:, c * P:(c + 1) * P], ident[0:self.rows, 0:self.rows])
        turn.then_inc(self.turned.sem, 1)


def make_identity(g, ident, done, first):
    g.memset(ident[:, :], 0.0).then_inc(done.sem, 1)
    g.wait_ge(done.sem, done.at(0, first + 1))
    g.affine_select(out=ident[:, :], in_=ident[:, :], compare_op=ALU.not_equal, fill=1.0, base=0,
                            pattern=[[-1, ident.shape[1]]], channel_multiplier=1).then_inc(done.sem, 1)


def make_selector(g, sel, done):
    g.memset(sel[:, :, :], 0.0).then_inc(done.sem, 1)
    g.wait_ge(done.sem, done.at(0, 1))
    g.affine_select(out=sel[:, :, :], in_=sel[:, :, :], compare_op=ALU.not_equal, fill=1.0, base=0,
                            pattern=[[-1, sel.shape[1]], [0, P]], channel_multiplier=1).then_inc(done.sem, 1)
    g.wait_ge(done.sem, done.at(0, 2))


def context_attention(nc, K, x_in, x_out, A):
    H, D = 16, 16
    PAIRS = H // 2
    IMG_VER, TXT_VER = 0, 1
    UNITS = [(IMG_VER, 0, IMG)] + [(TXT_VER, IMG + TXT // 3 * n, TXT // 3) for n in range(3)]
    KEYS = [(IMG_VER, k, min(P, IMG - k)) for k in range(0, IMG, P)]
    KEYS += [(TXT_VER, IMG + k, min(P, TXT - k)) for k in range(0, TXT, P)]
    FIRST_TXT = sum(1 for kind, _, _ in KEYS if kind == IMG_VER)
    WIDE = max(n for _, _, n in UNITS)
    VALUES_BY_UNIT = {0: (0, 1), 1: (2, 3), 2: (4, 5), 3: (6, 7)}
    VALUES_BETWEEN = (8, 9, 10, 11)
    VALUES_BY_TRIAL = {10: 12, 20: 13}
    EARLY = 8
    with ExitStack() as ctx:
        S = Space(nc, ctx, "cross")
        wq = S.sb("wq", [P, CH, DIM])
        wk = S.sb("wk", [P, 2, CH, DIM])
        wv = S.sb("wv", [P, 2, CH, DIM])
        wo = S.sb("wo", [P, CH, DIM])
        bq = S.sb("bq", [1, DIM])
        bo = S.sb("bo", [1, DIM])
        bk = S.sb("bk", [P, 2, CH])
        bv = S.sb("bv", [P, 2, CH])
        bv_sum = S.sb("bv_sum", [P, CH])
        gq = S.sb("gq", [P, CH])
        gk = S.sb("gk", [P, 2, CH])
        parity = S.sb("parity", [P, 2])
        group = S.sb("group", [P, 4])
        slot = S.sb("slot", [P, 4, 2])
        gain = S.sb("gain", [P, 2, CH])
        slot_gain = S.sb("slot_gain", [P, 2, CH, 8])
        eps = S.sb("eps", [P, 1])
        sel = S.sb("sel", [P, 16, P], BF16)
        stack = S.sb("stack", [P, SEQ])
        position = S.sb("position", [1, TXT])
        key_index = S.sb("key_index", [P, len(KEYS) - FIRST_TXT])
        ones_row = S.sb("ones_row", [1, P], BF16)
        len_int = S.sb("len_int", [P, 1], I32)
        length = S.sb("length", [P, 1])
        flag = S.sb("flag", [P, 1])
        lift = S.sb("lift", [P, 1])
        mask_row = S.sb("mask_row", [1, TXT], BF16)
        key_bias = S.sb("key_bias", [P, len(KEYS) - FIRST_TXT])
        ctxT = S.sb("ctxT", [P, CH, CTX])
        q_square = S.sb("q_square", [SEQ, DIM])
        q_ss = S.sb("q_ss", [SEQ, 1])
        q_log = S.sb("q_log", [SEQ, 1])
        q_rstd = S.sb("q_rstd", [SEQ, 1])
        qn = S.sb("qn", [SEQ, DIM])
        q_slots = S.sb("q_slots", [P, 2, CH, 8, SEQ])
        q_low = S.sb("q_low", [P, 2, CH, 8, SEQ], BF16)
        k_sb = S.sb("k", [P, CH, CTX])
        k_low = S.sb("k_low", [P, CH, CTX], BF16)
        k_square = S.sb("k_square", [P, 2, CH, WIDE])
        k_log = S.sb("k_log", [P, 2, WIDE])
        k_rstd = S.sb("k_rstd", [P, 2, WIDE])
        v_sb = S.sb("v", [P, len(KEYS), PAIRS, 2 * D + 1])
        peaks = S.sb("peaks", [P, len(UNITS), PAIRS])
        neg_peak = S.sb("neg_peak", [P, P])
        peak_rows = S.sb("peak_rows", [P, P], BF16)
        prob = S.sb("prob", [P, 2, PAIRS, P])
        inv = S.sb("inv", [P, 2, PAIRS])
        attn = S.sb("attn", [P, 2, PAIRS, 2 * D])
        attnT = S.sb("attnT", [P, CH, SEQ])
        residual = S.sb("residual", [SEQ, DIM])
        y = S.sb("y", [SEQ, DIM])
        big_ps = S.ps("big_ps", [P, 4, 512])
        pv_ps = S.ps("pv_ps", [P, 2, 512])
        misc_ps = S.ps("misc_ps", [P, 2, 512])

        N = Norm(S, SEQ, misc_ps[:, 0, 0:CH * SEQ].rearrange("p (c k) -> p c k", c=CH))
        qT_ps = misc_ps[:, 0, 0:CH * SEQ].rearrange("p (c k) -> p c k", c=CH)
        LOADS = 15
        loaded = S.dma("loaded", per=LOADS)
        set_up = S.sig("set_up", per=16)
        set_up2 = S.sig("set_up2", per=2)
        sel_set = S.sig("sel_set", per=2)
        position_set = S.sig("position_set", per=2)
        ones_set = S.sig("ones_set", per=4)
        eps_set = S.sig("eps_set")
        paused = S.sig("paused")
        v_setup = S.sig("v_setup", per=7)
        len_loaded = S.dma("len_loaded")
        ctx_loaded = S.dma("ctx_loaded")
        residual_loaded = S.dma("residual_loaded")
        mask_steps = S.sig("mask_steps", per=6)
        q_done = S.sig("q_done")
        q_stat = S.sig("q_stat", per=3)
        qn_done = S.sig("qn_done")
        q_turned = S.sig("q_turned")
        q_slots_done = S.sig("q_slots_done", per=4)
        q_low_done = S.sig("q_low_done")
        k_done = S.sig("k_done", per=2 * len(UNITS))
        k_raw_done = S.sig("k_raw_done", per=2 * len(UNITS))
        ss_done = S.sig("ss_done", per=len(UNITS))
        k_log_done = S.sig("k_log_done", per=len(UNITS))
        k_rstd_done = S.sig("k_rstd_done", per=len(UNITS))
        k_normed = S.sig("k_normed", per=len(UNITS))
        k_low_done = S.sig("k_low_done", per=len(UNITS))
        v_done = S.sig("v_done", per=len(KEYS))
        v_copied = S.sig("v_copied", per=EARLY)
        late_v_copied = S.sig("late_v_copied", per=len(KEYS) - EARLY)
        trial_done = S.sig("trial_done", per=PAIRS * len(UNITS))
        peak_done = S.sig("peak_done", per=PAIRS * len(UNITS))
        neg_peak_done = S.sig("neg_peak_done", per=2)
        peak_turned = S.sig("peak_turned")
        peak_rows_done = S.sig("peak_rows_done")
        score_done = S.sig("score_done", per=len(KEYS))
        prob_done = S.sig("prob_done", per=len(KEYS))
        pv_done = S.sig("pv_done", per=len(KEYS))
        inv_done = S.sig("inv_done", per=2)
        attn_done = S.sig("attn_done")
        attn_turned = S.sig("attn_turned")
        attnT_done = S.sig("attnT_done")
        out_done = S.sig("out_done")
        y_done = S.sig("y_done", credit=1)
        stored = S.dma("stored", credit=1)

        ctx_in = A["ctxT"].rearrange("b (c p) n -> b p c n", p=P)
        lens_in = A["lens"]

        with nc.Block() as block:
            @block.sync
            def _(sp):
                stored.open(sp)
                sp.dma_start(N.x[:, :], x_in[0]).then_inc(N.x_loaded.sem, 16)
                sp.dma_start(residual[:, :], x_in[0]).then_inc(residual_loaded.sem, 16)
                for kind, suffix in enumerate(("_img", "")):
                    sp.dma_start(wk[:, kind, :, :], A[f"L0_xattn_w_k{suffix}"].rearrange("(c p) n -> p c n", p=P)).then_inc(loaded.sem, 16)
                sp.dma_start(ctxT[:, :, :], ctx_in[0]).then_inc(ctx_loaded.sem, 16)
                for kind, suffix in enumerate(("_img", "")):
                    sp.dma_start(wv[:, kind, :, :], A[f"L0_xattn_w_v{suffix}"].rearrange("(c p) n -> p c n", p=P)).then_inc(loaded.sem, 16)
                    sp.dma_start(bk[:, kind, :], A[f"L0_xattn_b_k{suffix}"]).then_inc(loaded.sem, 16)
                    sp.dma_start(bv[:, kind, :], A[f"L0_xattn_b_v{suffix}"]).then_inc(loaded.sem, 16)
                    sp.dma_start(gk[:, kind, :], A[f"L0_xattn_g_k{suffix}"]).then_inc(loaded.sem, 16)
                sp.dma_start(wq[:, :, :], A["L0_xattn_w_q"].rearrange("(c p) n -> p c n", p=P)).then_inc(loaded.sem, 16)
                sp.dma_start(wo[:, :, :], A["L0_xattn_w_o"].rearrange("(c p) n -> p c n", p=P)).then_inc(loaded.sem, 16)
                sp.dma_start(bq[:, :], A["L0_xattn_b_q"]).then_inc(loaded.sem, 16)
                sp.dma_start(bo[:, :], A["L0_xattn_b_o"]).then_inc(loaded.sem, 16)
                sp.dma_start(gq[:, :], A["L0_xattn_g_q"]).then_inc(loaded.sem, 16)
                sp.dma_start(len_int[:, :], lens_in[0].broadcast_to([P, 1])).then_inc(len_loaded.sem, 16)
                with sp.Fori(0, BATCH - 1) as b:
                    sp.wait_ge(N.xn_done.sem, N.xn_done.at(b))
                    sp.dma_start(N.x[:, :], x_in[b + 1]).then_inc(N.x_loaded.sem, 16)
                    sp.wait_ge(k_done.sem, k_done.at(b, 2 * len(UNITS)))
                    sp.wait_ge(v_done.sem, v_done.at(b, len(KEYS)))
                    sp.dma_start(ctxT[:, :, :], ctx_in[b + 1]).then_inc(ctx_loaded.sem, 16)
                    sp.wait_ge(y_done.sem, y_done.at(b))
                    sp.dma_start(x_out[b], y[:, :]).then_inc(stored.sem, 16)
                    sp.dma_start(residual[:, :], x_in[b + 1]).then_inc(residual_loaded.sem, 16)
                    sp.dma_start(len_int[:, :], lens_in[b + 1].broadcast_to([P, 1])).then_inc(len_loaded.sem, 16)
                sp.wait_ge(N.xn_done.sem, N.xn_done.at(BATCH - 1))
                sp.sem_inc(N.x_loaded.sem, 16)
                sp.wait_ge(k_done.sem, k_done.at(BATCH - 1, 2 * len(UNITS)))
                sp.wait_ge(v_done.sem, v_done.at(BATCH - 1, len(KEYS)))
                sp.sem_inc(ctx_loaded.sem, 16)
                sp.wait_ge(y_done.sem, y_done.at(BATCH - 1))
                sp.dma_start(x_out[BATCH - 1], y[:, :]).then_inc(stored.sem, 16)
                sp.wait_ge(stored.sem, stored.before(BATCH))

            @block.gpsimd
            def _(g):
                make_parity(g, parity, set_up)
                count = 10
                for rows, cols, value in [(slice(0, P), slice(0, 4), 0.0)] + \
                        [(slice(32 * q, 32 * q + 32), slice(q, q + 1), 1.0) for q in range(4)]:
                    g.memset(group[rows, cols], value).then_inc(set_up.sem, 1)
                    count += 1
                    g.wait_ge(set_up.sem, set_up.at(0, count))
                g.memset(stack[:, :], 0.0).then_inc(set_up.sem, 1)
                for half in range(2):
                    g.wait_ge(set_up2.sem, set_up2.at(0, half)) if half else g.wait_ge(set_up.sem, set_up.at(0, 16))
                    g.affine_select(out=stack[:, :], in_=stack[:, :], compare_op=ALU.not_equal, fill=1.0,
                                               base=-SEQ * half, pattern=[[-1, SEQ]], channel_multiplier=1).then_inc(set_up2.sem, 1)
                g.wait_ge(set_up2.sem, set_up2.at(0, 2))
                make_selector(g, sel, sel_set)
                g.iota(position[:, :], pattern=[[1, TXT]], base=0, channel_multiplier=0,
                                       allow_small_or_imprecise_dtypes=True).then_inc(position_set.sem, 1)
                g.iota(key_index[:, :], pattern=[[P, len(KEYS) - FIRST_TXT]], base=0,
                                       channel_multiplier=1, allow_small_or_imprecise_dtypes=True).then_inc(position_set.sem, 1)
                g.wait_ge(position_set.sem, position_set.at(0, 2))
                g.memset(ones_row[:, :], 1.0).then_inc(ones_set.sem, 1)
                g.wait_ge(ones_set.sem, ones_set.at(0, 1))
                g.memset(v_sb[:, :, :, 2 * D:], 1.0).then_inc(ones_set.sem, 1)
                g.wait_ge(ones_set.sem, ones_set.at(0, 2))
                g.memset(attn[:, :, :, :], 0.0).then_inc(ones_set.sem, 1)
                g.wait_ge(ones_set.sem, ones_set.at(0, 3))
                g.memset(neg_peak[:, :], 0.0).then_inc(ones_set.sem, 1)

            @block.scalar
            def _(a):
                a.preload_act_table_set("natural_log_exp_and_others")
                a.wait_ge(N.eps_set.sem, N.eps_set.at(0))
                a.wait_ge(eps_set.sem, eps_set.at(0))
                a.wait_ge(loaded.sem, loaded.at(0, LOADS))
                N.scalar(a, 0)
                with a.Fori(0, BATCH) as b:

                    def k_unit(u):
                        kind, lo, n = UNITS[u]
                        for c in range(CH):
                            a.wait_ge(k_done.sem, k_done.at(b, 2 * u + c + 1))
                            a.activation(k_sb[:, c, lo:lo + n], big_ps[:, (2 * u + c) % 2, 0:n], ACT.Identity,
                                         bias=bk[:, kind, c:c + 1])
                            a.activation(k_square[:, u % 2, c, 0:n], big_ps[:, (2 * u + c) % 2, 0:n],
                                                       ACT.Square, bias=bk[:, kind, c:c + 1]).then_inc(k_raw_done.sem, 1)

                    def k_power(u):
                        kind, lo, n = UNITS[u]
                        a.wait_ge(ss_done.sem, ss_done.at(b, u + 1))
                        a.activation(k_log[:, u % 2, 0:n], big_ps[:, 2 + u % 2, 0:n], ACT.Ln,
                                                   scale=1.0 / DIM, bias=eps[:, 0:1]).then_inc(k_log_done.sem, 1)
                        a.wait_ge(k_log_done.sem, k_log_done.at(b, u + 1))
                        if u >= 2:
                            a.wait_ge(k_normed.sem, k_normed.at(b, u - 1))
                        a.activation(k_rstd[:, u % 2, 0:n], k_log[:, u % 2, 0:n], ACT.Exp, scale=-0.5).then_inc(k_rstd_done.sem, 1)

                    def k_lower(u):
                        kind, lo, n = UNITS[u]
                        a.wait_ge(k_normed.sem, k_normed.at(b, u + 1))
                        a.copy(k_low[:, :, lo:lo + n], k_sb[:, :, lo:lo + n]).then_inc(k_low_done.sem, 1)

                    def copy_values(j):
                        kind, lo, n = KEYS[j]
                        a.wait_ge(v_done.sem, v_done.at(b, j + 1))
                        a.copy(v_sb[0:n, j, :, 0:2 * D],
                               pv_ps[0:n, j % 2, 0:DIM].rearrange("p (i d) -> p i d", d=2 * D)).then_inc(late_v_copied.sem, 1)

                    k_unit(0)
                    a.wait_ge(q_done.sem, q_done.at(b))
                    a.activation(q_square[:, :], misc_ps[0:SEQ, 1, 0:DIM], ACT.Square, accum_out=q_ss[:, :]).then_inc(q_stat.sem, 1)
                    a.wait_ge(q_stat.sem, q_stat.at(b, 1))
                    a.activation(q_log[:, :], q_ss[:, :], ACT.Ln, scale=1.0 / DIM, bias=eps[0:SEQ, 0:1]).then_inc(q_stat.sem, 1)
                    a.wait_ge(q_stat.sem, q_stat.at(b, 2))
                    a.activation(q_rstd[:, :], q_log[:, :], ACT.Exp, scale=-0.5).then_inc(q_stat.sem, 1)
                    for u in range(len(UNITS)):
                        if u + 1 < len(UNITS):
                            k_unit(u + 1)
                        if u >= 1:
                            k_lower(u - 1)
                        k_power(u)
                    copy_values(EARLY)
                    copy_values(EARLY + 1)
                    k_lower(len(UNITS) - 1)
                    for j in range(EARLY + 2, len(KEYS)):
                        copy_values(j)
                    for j, (kind, lo, n) in enumerate(KEYS):
                        a.wait_ge(score_done.sem, score_done.at(b, j + 1))
                        if j >= 2:
                            a.wait_ge(pv_done.sem, pv_done.at(b, j - 1))
                        bias = 0.0 if kind == IMG_VER else key_bias[0:n, j - FIRST_TXT:j - FIRST_TXT + 1]
                        if j == FIRST_TXT:
                            a.wait_ge(mask_steps.sem, mask_steps.at(b, 6))
                        both = 2 * (j % 2)
                        a.activation(prob[0:n, j % 2, :, :],
                                                  big_ps[0:n, both:both + 2, :].rearrange("p c (g k) -> p (c g) k", g=4),
                                                  ACT.Exp, bias=bias).then_inc(prob_done.sem, 1)
                        if j == 3:
                            N.scalar(a, b + 1)

            @block.tensor
            def _(pe):
                pe.wait_ge(loaded.sem, loaded.at(0, LOADS))
                pe.wait_ge(set_up2.sem, set_up2.at(0, 2))
                pe.wait_ge(sel_set.sem, sel_set.at(0, 2))
                pe.wait_ge(ones_set.sem, ones_set.at(0, 4))

                def k_unit(b, u, chunks=range(CH)):
                    kind, lo, n = UNITS[u]
                    for c in chunks:
                        if 2 * u + c >= 2:
                            pe.wait_ge(k_raw_done.sem, k_raw_done.at(b, 2 * u + c - 1))
                        for m in range(CH):
                            mm = pe.matmul(big_ps[:, (2 * u + c) % 2, 0:n], wk[:, kind, m, c * P:(c + 1) * P],
                                           ctxT[:, m, lo:lo + n], start=(m == 0), stop=(m == CH - 1))
                        mm.then_inc(k_done.sem, 1)

                pe.wait_ge(ctx_loaded.sem, ctx_loaded.at(0))
                N.tensor(pe, 0, K.ident)
                k_unit(0, 0)
                with pe.Fori(0, BATCH) as b:
                    def square_sums(u):
                        kind, lo, n = UNITS[u]
                        pe.wait_ge(k_raw_done.sem, k_raw_done.at(b, 2 * u + 2))
                        if u >= 2:
                            pe.wait_ge(k_log_done.sem, k_log_done.at(b, u - 1))
                        for c in range(CH):
                            mm = pe.matmul(big_ps[:, 2 + u % 2, 0:n], K.ones[:, :], k_square[:, u % 2, c, 0:n],
                                           start=(c == 0), stop=(c == CH - 1))
                        mm.then_inc(ss_done.sem, 1)

                    def values(j):
                        kind, lo, n = KEYS[j]
                        if j >= 2:
                            if j - 2 < EARLY:
                                pe.wait_ge(v_copied.sem, v_copied.at(b, j - 1))
                            else:
                                pe.wait_ge(late_v_copied.sem, late_v_copied.at(b, j - 1 - EARLY))
                        for m in range(CH):
                            mm = pe.matmul(pv_ps[0:n, j % 2, 0:DIM], ctxT[:, m, lo:lo + n], wv[:, kind, m, :],
                                           start=(m == 0), stop=(m == CH - 1))
                        mm.then_inc(v_done.sem, 1)

                    pe.wait_ge(y_done.sem, y_done.before(b))
                    pe.wait_ge(N.xnT_done.sem, N.xnT_done.at(b))
                    for c in range(CH):
                        pe.matmul(misc_ps[0:SEQ, 1, 0:DIM], N.xnT[:, c, :], wq[:, c, :], start=(c == 0), stop=False)
                    pe.matmul(misc_ps[0:SEQ, 1, 0:DIM], K.ones[0:1, 0:SEQ], bq[0:1, :], start=False, stop=True).then_inc(q_done.sem, 1)
                    for u in range(len(UNITS)):
                        if u + 1 < len(UNITS):
                            k_unit(b, u + 1)
                        for j in VALUES_BY_UNIT[u]:
                            values(j)
                        square_sums(u)
                        if u == 1:
                            pe.wait_ge(qn_done.sem, qn_done.at(b))
                            pe.sem_inc(paused.sem, 1)
                            for c in range(CH):
                                turn = pe.transpose(qT_ps[:, c, :], qn[:, c * P:(c + 1) * P], K.ident[0:SEQ, 0:SEQ])
                            turn.then_inc(q_turned.sem, 1)
                    for j in VALUES_BETWEEN:
                        values(j)
                    pe.wait_ge(q_low_done.sem, q_low_done.at(b))
                    pe.wait_ge(k_low_done.sem, k_low_done.at(b, len(UNITS)))
                    pe.wait_ge(mask_steps.sem, mask_steps.at(b, 6))
                    for i in range(PAIRS):
                        for u, (kind, lo, n) in enumerate(UNITS):
                            m = i * len(UNITS) + u
                            if m >= 4:
                                pe.wait_ge(peak_done.sem, peak_done.at(b, m - 3))
                            c, g = i // 4, i % 4
                            mm = pe.matmul(big_ps[:, m % 4, 0:n], q_low[:, kind, c, 2 * g:2 * g + 2, :],
                                           k_low[:, c, lo:lo + n], start=True, stop=(kind == IMG_VER))
                            if kind == TXT_VER:
                                mm = pe.matmul(big_ps[:, m % 4, 0:n], ones_row[0:1, :], mask_row[0:1, lo - IMG:lo - IMG + n],
                                               start=False, stop=True)
                            mm.then_inc(trial_done.sem, 1)
                            if m in VALUES_BY_TRIAL:
                                values(VALUES_BY_TRIAL[m])
                    pe.wait_ge(neg_peak_done.sem, neg_peak_done.at(b, 2))
                    pe.transpose(misc_ps[:, 0, 0:P], neg_peak[:, :], K.ident[:, :]).then_inc(peak_turned.sem, 1)
                    pe.wait_ge(peak_rows_done.sem, peak_rows_done.at(b))
                    pe.wait_ge(late_v_copied.sem, late_v_copied.at(b, len(KEYS) - EARLY))

                    def scores(j):
                        kind, lo, n = KEYS[j]
                        if j >= 2:
                            pe.wait_ge(prob_done.sem, prob_done.at(b, j - 1))
                        for c in range(CH):
                            bank = big_ps[0:n, 2 * (j % 2) + c, :]
                            pe.matmul(bank, k_sb[:, c, lo:lo + n], q_slots[:, kind, c, :, :], start=True, stop=False,
                                      skip_group_check=True)
                            for g in range(4):
                                mm = pe.matmul(bank[:, g * P:(g + 1) * P], sel[:, 8 * kind + 4 * c + g, 0:n],
                                               peak_rows[:, :], start=False, stop=(g == 3), skip_group_check=True)
                        mm.then_inc(score_done.sem, 1)

                    def weigh(j):
                        kind, lo, n = KEYS[j]
                        pe.wait_ge(prob_done.sem, prob_done.at(b, j + 1))
                        first = j == 0 or j == FIRST_TXT
                        for i in range(PAIRS):
                            mm = pe.matmul(pv_ps[:, kind, i * 33:i * 33 + 33], prob[0:n, j % 2, i, :], v_sb[0:n, j, i, :],
                                           start=(first and i == 0), stop=(j in (FIRST_TXT - 1, len(KEYS) - 1)),
                                           skip_group_check=True)
                        mm.then_inc(pv_done.sem, 1)

                    scores(0)
                    for j in range(len(KEYS)):
                        if j + 1 < len(KEYS):
                            scores(j + 1)
                        weigh(j)
                        if j == 6:
                            N.tensor(pe, b + 1, K.ident)
                    pe.wait_ge(ctx_loaded.sem, ctx_loaded.at(b + 1))
                    k_unit(b + 1, 0, [0])
                    pe.wait_ge(attn_done.sem, attn_done.at(b))
                    for c in range(CH):
                        for kind in range(2):
                            mm = pe.matmul(misc_ps[:, 0, c * SEQ:(c + 1) * SEQ],
                                           attn[:, kind, 4 * c:4 * c + 4, :], stack[:, :],
                                           start=(kind == 0), stop=(kind == 1))
                    mm.then_inc(attn_turned.sem, 1)
                    k_unit(b + 1, 0, [1])
                    pe.wait_ge(attnT_done.sem, attnT_done.at(b))
                    for c in range(CH):
                        pe.matmul(misc_ps[0:SEQ, 1, 0:DIM], attnT[:, c, :], wo[:, c, :], start=(c == 0), stop=False)
                    pe.matmul(misc_ps[0:SEQ, 1, 0:DIM], K.ones[0:1, 0:SEQ], bo[0:1, :], start=False, stop=True).then_inc(out_done.sem, 1)

            @block.vector
            def _(v):
                N.setup_vector(v)
                v.memset(eps[:, :], 1e-6).then_inc(eps_set.sem, 1)
                y_done.open(v)
                v.wait_ge(loaded.sem, loaded.at(0, LOADS))
                v.wait_ge(set_up.sem, set_up.at(0, 15))
                v.wait_ge(position_set.sem, position_set.at(0, 2))
                v.wait_ge(ones_set.sem, ones_set.at(0, 4))
                v.tensor_tensor(slot[:, :, :], group[:, :].unsqueeze(2).broadcast_to([P, 4, 2]),
                                           parity[:, :].unsqueeze(1).broadcast_to([P, 4, 2]), ALU.mult).then_inc(v_setup.sem, 1)
                v.scalar_tensor_tensor(gain[:, :, :], gk[:, :, :], float(D) ** -0.5,
                                                  gq[:, :].unsqueeze(1).broadcast_to([P, 2, CH]), ALU.mult, ALU.mult).then_inc(v_setup.sem, 1)
                v.tensor_tensor(bv_sum[:, :], bv[:, 0, :], bv[:, 1, :], ALU.add).then_inc(v_setup.sem, 1)
                v.wait_ge(v_setup.sem, v_setup.at(0, 3))
                for kind in range(2):
                    for c in range(CH):
                        v.tensor_scalar(slot_gain[:, kind, c, :], slot[:, :, :].rearrange("p g r -> p (g r)"),
                                                   gain[:, kind, c:c + 1], None, ALU.mult).then_inc(v_setup.sem, 1)
                v.wait_ge(v_setup.sem, v_setup.at(0, 7))
                N.vector(v, 0)
                with v.Fori(0, BATCH) as b:
                    v.wait_ge(len_loaded.sem, len_loaded.at(b))
                    v.tensor_copy(length[:, :], len_int[:, :]).then_inc(mask_steps.sem, 1)
                    v.wait_ge(mask_steps.sem, mask_steps.at(b, 1))
                    v.tensor_scalar(flag[:, :], length[:, :], 0.5, None, ALU.is_gt).then_inc(mask_steps.sem, 1)
                    v.tensor_scalar(lift[:, :], length[:, :], 0.5, 1e9, ALU.is_lt, ALU.mult).then_inc(mask_steps.sem, 1)
                    v.wait_ge(mask_steps.sem, mask_steps.at(b, 3))
                    v.tensor_tensor(length[:, :], length[:, :], lift[:, :], ALU.add).then_inc(mask_steps.sem, 1)
                    v.wait_ge(mask_steps.sem, mask_steps.at(b, 4))
                    v.tensor_scalar(mask_row[:, :], position[:, :], length[0:1, 0:1], NEG, ALU.is_ge, ALU.mult).then_inc(mask_steps.sem, 1)
                    v.tensor_scalar(key_bias[:, :], key_index[:, :], length[:, 0:1], NEG, ALU.is_ge, ALU.mult).then_inc(mask_steps.sem, 1)

                    def copy_values(j):
                        kind, lo, n = KEYS[j]
                        v.wait_ge(v_done.sem, v_done.at(b, j + 1))
                        v.tensor_copy(v_sb[0:n, j, :, 0:2 * D],
                                                  pv_ps[0:n, j % 2, 0:DIM].rearrange("p (i d) -> p i d", d=2 * D)).then_inc(v_copied.sem, 1)

                    for u, (kind, lo, n) in enumerate(UNITS):
                        for j in VALUES_BY_UNIT[u]:
                            copy_values(j)
                        v.wait_ge(k_rstd_done.sem, k_rstd_done.at(b, u + 1))
                        for c in range(CH):
                            if kind == IMG_VER:
                                last = v.tensor_tensor(k_sb[:, c, lo:lo + n], k_sb[:, c, lo:lo + n],
                                                       k_rstd[:, u % 2, 0:n], ALU.mult)
                            else:
                                last = v.scalar_tensor_tensor(k_sb[:, c, lo:lo + n], k_sb[:, c, lo:lo + n], flag[:, 0:1],
                                                              k_rstd[:, u % 2, 0:n], ALU.mult, ALU.mult)
                        last.then_inc(k_normed.sem, 1)
                        if u == 0:
                            v.wait_ge(q_stat.sem, q_stat.at(b, 3))
                            v.tensor_scalar(qn[:, :], misc_ps[0:SEQ, 1, 0:DIM], q_rstd[:, 0:1], None, ALU.mult).then_inc(qn_done.sem, 1)
                        if u == 2:
                            v.wait_ge(q_turned.sem, q_turned.at(b))
                            for kind in range(2):
                                for c in range(CH):
                                    v.tensor_tensor(
                                        q_slots[:, kind, c, :, :], qT_ps[:, c, :].unsqueeze(1).broadcast_to([P, 8, SEQ]),
                                        slot_gain[:, kind, c, :].unsqueeze(2).broadcast_to([P, 8, SEQ]), ALU.mult).then_inc(q_slots_done.sem, 1)
                            v.wait_ge(q_slots_done.sem, q_slots_done.at(b, 4))
                            v.tensor_copy(q_low[:, :, :, :, :], q_slots[:, :, :, :, :]).then_inc(q_low_done.sem, 1)
                    for i in range(PAIRS):
                        for u, (kind, lo, n) in enumerate(UNITS):
                            m = i * len(UNITS) + u
                            v.wait_ge(trial_done.sem, trial_done.at(b, m + 1))
                            v.tensor_reduce(peaks[:, u, i:i + 1], big_ps[:, m % 4, 0:n], AX.X, ALU.max).then_inc(peak_done.sem, 1)
                    v.wait_ge(peak_done.sem, peak_done.at(b, PAIRS * len(UNITS)))
                    v.tensor_scalar(neg_peak[:, 0:8], peaks[:, 0, :], -1.0, None, ALU.mult).then_inc(neg_peak_done.sem, 1)
                    v.tensor_reduce(neg_peak[:, 8:16], peaks[:, 1:4, :].rearrange("p u i -> p i u"),
                                                     AX.X, ALU.max, negate=True).then_inc(neg_peak_done.sem, 1)
                    v.wait_ge(peak_turned.sem, peak_turned.at(b))
                    v.tensor_copy(peak_rows[:, :], misc_ps[:, 0, 0:P]).then_inc(peak_rows_done.sem, 1)
                    N.vector(v, b + 1)
                    for kind, last in ((IMG_VER, FIRST_TXT), (TXT_VER, len(KEYS))):
                        v.wait_ge(pv_done.sem, pv_done.at(b, last))
                        sums = pv_ps[:, kind, 0:PAIRS * 33].rearrange("p (i d) -> p i d", d=33)
                        v.reciprocal(inv[:, kind, :], sums[:, :, 32]).then_inc(inv_done.sem, 1)
                        v.wait_ge(inv_done.sem, inv_done.at(b, kind + 1))
                        for par in range(2):
                            rows, cols = slice(par * SEQ, par * SEQ + SEQ), slice(par * D, par * D + D)
                            mul = v.tensor_tensor(attn[rows, kind, :, cols], sums[rows, :, cols],
                                                  inv[rows, kind, :].unsqueeze(2).broadcast_to([SEQ, PAIRS, D]), ALU.mult)
                    mul.then_inc(attn_done.sem, 1)
                    v.wait_ge(attn_turned.sem, attn_turned.at(b))
                    for c in range(CH):
                        copy = v.tensor_scalar(attnT[:, c, :], misc_ps[:, 0, c * SEQ:(c + 1) * SEQ], bv_sum[:, c:c + 1],
                                               None, ALU.add)
                    copy.then_inc(attnT_done.sem, 1)
                    v.wait_ge(out_done.sem, out_done.at(b))
                    v.wait_ge(stored.sem, stored.before(b))
                    v.wait_ge(residual_loaded.sem, residual_loaded.at(b))
                    v.tensor_tensor(y[:, :], misc_ps[0:SEQ, 1, 0:DIM], residual[:, :], ALU.add).then_inc(y_done.sem, 1)
        S.clear()




def context_gqa(nc, K, x_in, x_out, A):
    H, KV, D = 16, 4, 128
    HALF = D // 2
    PAIRS = H // 2
    ALL = CTX + SEQ
    CUTS = [0, 417, 833, 1249, ALL]
    COLS = list(zip(CUTS[:-1], CUTS[1:]))
    WIDE = 512
    KEYS = [(k, min(P, ALL - k)) for k in range(0, ALL, P)]
    K_UNITS = KV * len(COLS)
    Q_UNITS = 2
    UNITS = K_UNITS + Q_UNITS
    VALUES_BY_UNIT = {0: 0, 4: 1, 8: 2, 12: 3, 16: 4}
    VALUES_BETWEEN = (5, 6, 7, 8)
    VALUES_BY_TRIAL = {15: 9, 18: 10, 21: 11, 24: 12, 27: 13}
    QH = H // Q_UNITS
    TWO_PI_HIGH = 6.28125
    TWO_PI_LOW = float(2 * np.pi - 6.28125)
    ROUND = 1.5 * 2.0 ** 23
    PI_BELOW = float(np.nextafter(np.float32(np.pi), np.float32(0)))
    with ExitStack() as ctx:
        S = Space(nc, ctx, "gqa")
        wq = S.sb("wq", [P, CH, H * D])
        wk = S.sb("wk", [P, CH, KV * D])
        wv = S.sb("wv", [P, CH, KV * D])
        wo = S.sb("wo", [P, H, DIM])
        norm_w = S.sb("norm_w", [P, 2])
        inv_freq = S.sb("inv_freq", [P, 1])
        sign = S.sb("sign", [P, 1])
        half_pi = S.sb("half_pi", [P, 1])
        eps = S.sb("eps", [P, 1])
        sel = S.sb("sel", [P, PAIRS, P], BF16)
        ctxT = S.sb("ctxT", [P, CH, ALL])
        pos = S.sb("pos", [P, ALL], I32)
        angle = S.sb("angle", [P, ALL])
        turns = S.sb("turns", [P, ALL])
        cos = S.sb("cos", [P, ALL])
        sin = S.sb("sin", [P, ALL])
        square = S.sb("square", [P, 2, WIDE])
        log = S.sb("log", [P, WIDE])
        rstd = S.sb("rstd", [P, 2, WIDE])
        normed = S.sb("normed", [P, 2, WIDE])
        by_cos = S.sb("by_cos", [P, 2, WIDE])
        by_sin = S.sb("by_sin", [P, 2, WIDE])
        k_sb = S.sb("k", [P, KV, ALL])
        k_low = S.sb("k_low", [P, KV, ALL], BF16)
        q_sb = S.sb("q", [P, H, SEQ])
        q_low = S.sb("q_low", [P, H, SEQ], BF16)
        v_sb = S.sb("v", [P, len(KEYS), KV, D + 1])
        peaks = S.sb("peaks", [P, len(COLS), PAIRS])
        neg_peak = S.sb("neg_peak", [P, P])
        peak_rows = S.sb("peak_rows", [P, P], BF16)
        prob = S.sb("prob", [P, 2, PAIRS, P])
        inv = S.sb("inv", [P, PAIRS])
        attn = prob[:, 0, :, :]
        attnT = prob[:, 1, :, :]
        residual = S.sb("residual", [SEQ, DIM])
        y = S.sb("y", [SEQ, DIM])
        big_ps = S.ps("big_ps", [P, 4, 512])
        pv_ps = S.ps("pv_ps", [P, 3, 512])
        misc_ps = S.ps("misc_ps", [P, 512])
        turned_ps = [big_ps[:, 3, :], pv_ps[:, 2, :]]

        N = Norm(S, SEQ, misc_ps[:, 0:CH * SEQ].rearrange("p (c k) -> p c k", c=CH))
        LOADS = 9
        loaded = S.dma("loaded", per=LOADS)
        sel_set = S.sig("sel_set", per=2)
        consts_set = S.sig("consts_set", per=4)
        ones_set = S.sig("ones_set", per=2)
        paused = S.sig("paused")
        ctx_loaded = S.dma("ctx_loaded")
        residual_loaded = S.dma("residual_loaded")
        pos_loaded = S.dma("pos_loaded", per=2)
        angle_steps = S.sig("angle_steps", per=6)
        table_done = S.sig("table_done", per=3)
        tail_done = S.sig("tail_done")
        unit_done = S.sig("unit_done", per=UNITS)
        square_done = S.sig("square_done", per=UNITS)
        ss_done = S.sig("ss_done", per=UNITS)
        log_done = S.sig("log_done", per=UNITS)
        rstd_done = S.sig("rstd_done", per=UNITS)
        normed_done = S.sig("normed_done", per=UNITS)
        by_sin_done = S.sig("by_sin_done", per=UNITS)
        by_cos_done = S.sig("by_cos_done", per=UNITS)
        rope_done = S.sig("rope_done", per=UNITS)
        low_done = S.sig("low_done", per=UNITS)
        v_done = S.sig("v_done", per=len(KEYS))
        v_copied = S.sig("v_copied", per=len(KEYS))
        trial_done = S.sig("trial_done", per=PAIRS * len(COLS))
        peak_done = S.sig("peak_done", per=PAIRS * len(COLS))
        neg_peak_done = S.sig("neg_peak_done")
        peak_turned = S.sig("peak_turned")
        peak_rows_done = S.sig("peak_rows_done")
        score_done = S.sig("score_done", per=len(KEYS))
        prob_done = S.sig("prob_done", per=len(KEYS))
        pv_done = S.sig("pv_done", per=len(KEYS))
        inv_done = S.sig("inv_done")
        attn_done = S.sig("attn_done")
        attn_turned = S.sig("attn_turned", per=2)
        attnT_done = S.sig("attnT_done", per=2)
        out_done = S.sig("out_done")
        y_done = S.sig("y_done", credit=1)
        stored = S.dma("stored", credit=1)

        ctx_in = A["ctxT"].rearrange("b (c p) n -> b p c n", p=P)

        def unit_views(n):
            if n < K_UNITS:
                g, (lo, hi) = n // len(COLS), COLS[n % len(COLS)]
                return (hi - lo, 0, lambda ap: ap[:, 0:hi - lo], lambda table: table[:, lo:hi],
                        k_sb[:, g, lo:hi], k_low[:, g, lo:hi])
            h = (n - K_UNITS) * QH
            return (QH * SEQ, 1, lambda ap: ap[:, 0:QH * SEQ].rearrange("p (h k) -> p h k", h=QH),
                    lambda table: table[:, CTX:ALL].unsqueeze(1).broadcast_to([table.shape[0], QH, SEQ]),
                    q_sb[:, h:h + QH, :], q_low[:, h:h + QH, :])

        with nc.Block() as block:
            @block.sync
            def _(sp):
                stored.open(sp)
                sp.dma_start(N.x[:, :], x_in[0]).then_inc(N.x_loaded.sem, 16)

                def load_positions(b):
                    sp.dma_start(pos[:, 0:CTX], A["pos"][b].broadcast_to([P, CTX])).then_inc(pos_loaded.sem, 16)
                    sp.dma_start(pos[:, CTX:ALL], A["draft_pos"][b].broadcast_to([P, SEQ])).then_inc(pos_loaded.sem, 16)

                load_positions(0)
                sp.dma_start(residual[:, :], x_in[0]).then_inc(residual_loaded.sem, 16)
                sp.dma_start(inv_freq[:, :], A["gqa_inv_freq"]).then_inc(loaded.sem, 16)
                sp.dma_start(sign[:, :], A["gqa_sign"]).then_inc(loaded.sem, 16)
                sp.dma_start(wk[:, :, :], A["L1_xattn_Wk"].rearrange("(c p) n -> p c n", p=P)).then_inc(loaded.sem, 16)
                sp.dma_start(ctxT[:, :, 0:CTX], ctx_in[0]).then_inc(ctx_loaded.sem, 16)
                sp.dma_start(norm_w[:, 0:1], A["L1_xattn_k_norm_w"]).then_inc(loaded.sem, 16)
                sp.dma_start(norm_w[:, 1:2], A["L1_xattn_q_norm_w"]).then_inc(loaded.sem, 16)
                sp.dma_start(wv[:, :, :], A["L1_xattn_Wv"].rearrange("(c p) n -> p c n", p=P)).then_inc(loaded.sem, 16)
                for c in range(CH):
                    sp.dma_start(wq[:, c, :], A["L1_xattn_Wq"][c * P:(c + 1) * P, :]).then_inc(loaded.sem, 16)
                sp.dma_start(wo[:, :, :], A["L1_xattn_Wo"].rearrange("(h p) n -> p h n", p=P)).then_inc(loaded.sem, 16)
                with sp.Fori(0, BATCH - 1) as b:
                    sp.wait_ge(N.xn_done.sem, N.xn_done.at(b))
                    sp.dma_start(N.x[:, :], x_in[b + 1]).then_inc(N.x_loaded.sem, 16)
                    sp.wait_ge(angle_steps.sem, angle_steps.at(b, 1))
                    load_positions(b + 1)
                    sp.wait_ge(unit_done.sem, unit_done.at(b, K_UNITS))
                    sp.wait_ge(v_done.sem, v_done.at(b, len(KEYS)))
                    sp.dma_start(ctxT[:, :, 0:CTX], ctx_in[b + 1]).then_inc(ctx_loaded.sem, 16)
                    sp.wait_ge(y_done.sem, y_done.at(b))
                    sp.dma_start(x_out[b], y[:, :]).then_inc(stored.sem, 16)
                    sp.dma_start(residual[:, :], x_in[b + 1]).then_inc(residual_loaded.sem, 16)
                sp.wait_ge(N.xn_done.sem, N.xn_done.at(BATCH - 1))
                sp.sem_inc(N.x_loaded.sem, 16)
                sp.wait_ge(angle_steps.sem, angle_steps.at(BATCH - 1, 1))
                load_positions(0)
                sp.wait_ge(unit_done.sem, unit_done.at(BATCH - 1, K_UNITS))
                sp.wait_ge(v_done.sem, v_done.at(BATCH - 1, len(KEYS)))
                sp.sem_inc(ctx_loaded.sem, 16)
                sp.wait_ge(y_done.sem, y_done.at(BATCH - 1))
                sp.dma_start(x_out[BATCH - 1], y[:, :]).then_inc(stored.sem, 16)
                sp.wait_ge(stored.sem, stored.before(BATCH))

            @block.gpsimd
            def _(g):
                make_selector(g, sel, sel_set)
                g.memset(v_sb[:, :, :, D:D + 1], 1.0).then_inc(ones_set.sem, 1)
                g.wait_ge(ones_set.sem, ones_set.at(0, 1))
                g.memset(neg_peak[:, :], 0.0).then_inc(ones_set.sem, 1)
                with g.Fori(0, BATCH) as b:
                    for n in range(UNITS):
                        width, which, view, table, exact, low = unit_views(n)
                        g.wait_ge(normed_done.sem, normed_done.at(b, n + 1))
                        if n >= 2:
                            g.wait_ge(rope_done.sem, rope_done.at(b, n - 1))
                        g.tensor_tensor(view(by_cos[:, n % 2, :]), view(normed[:, n % 2, :]), table(cos), ALU.mult).then_inc(by_cos_done.sem, 1)
                        g.wait_ge(by_sin_done.sem, by_sin_done.at(b, n + 1))
                        g.wait_ge(by_cos_done.sem, by_cos_done.at(b, n + 1))
                        g.tensor_tensor(exact, view(by_cos[:, n % 2, :]), view(by_sin[:, n % 2, :]), ALU.add).then_inc(rope_done.sem, 1)

            @block.scalar
            def _(a):
                def tables(b, wait_use):
                    a.wait_ge(angle_steps.sem, angle_steps.at(b, 6))
                    if wait_use:
                        a.wait_ge(by_sin_done.sem, by_sin_done.at(b - 1, UNITS))
                        a.wait_ge(by_cos_done.sem, by_cos_done.at(b - 1, UNITS))
                    a.activation(sin[:, :], angle[:, :], ACT.Sin, scale=sign[:, 0:1]).then_inc(table_done.sem, 1)
                    a.activation(turns[:, :], angle[:, :], ACT.Abs).then_inc(table_done.sem, 1)
                    a.wait_ge(table_done.sem, table_done.at(b, 2))
                    a.activation(cos[:, :], turns[:, :], ACT.Sin, scale=-1.0, bias=half_pi[:, 0:1]).then_inc(table_done.sem, 1)
                    a.preload_act_table_set("natural_log_exp_and_others")

                a.wait_ge(N.eps_set.sem, N.eps_set.at(0))
                a.wait_ge(consts_set.sem, consts_set.at(0, 4))
                a.wait_ge(loaded.sem, loaded.at(0, LOADS))
                tables(0, False)
                N.scalar(a, 0)
                with a.Fori(0, BATCH) as b:
                    def squares(n):
                        width = unit_views(n)[0]
                        a.wait_ge(unit_done.sem, unit_done.at(b, n + 1))
                        if n >= 2:
                            a.wait_ge(ss_done.sem, ss_done.at(b, n - 1))
                        a.activation(square[:, n % 2, 0:width], big_ps[:, n % 3, 0:width], ACT.Square).then_inc(square_done.sem, 1)

                    def copy_values(j):
                        lo, n = KEYS[j]
                        a.wait_ge(v_done.sem, v_done.at(b, j + 1))
                        a.copy(v_sb[0:n, j, :, 0:D], pv_ps[0:n, j % 2, :].rearrange("p (g d) -> p g d", g=KV)).then_inc(v_copied.sem, 1)

                    def power(n):
                        width = unit_views(n)[0]
                        sums = big_ps[:, 3, 0:width] if n % 2 == 0 else pv_ps[:, 2, 0:width]
                        a.wait_ge(ss_done.sem, ss_done.at(b, n + 1))
                        if n >= 1:
                            a.wait_ge(rstd_done.sem, rstd_done.at(b, n))
                        a.activation(log[:, 0:width], sums, ACT.Ln, scale=1.0 / D, bias=eps[:, 0:1]).then_inc(log_done.sem, 1)
                        a.wait_ge(log_done.sem, log_done.at(b, n + 1))
                        if n >= 2:
                            a.wait_ge(normed_done.sem, normed_done.at(b, n - 1))
                        a.activation(rstd[:, n % 2, 0:width], log[:, 0:width], ACT.Exp, scale=-0.5).then_inc(rstd_done.sem, 1)

                    squares(0)
                    for n in range(UNITS):
                        if n + 1 < UNITS:
                            squares(n + 1)
                        if n in VALUES_BY_UNIT:
                            copy_values(VALUES_BY_UNIT[n])
                        power(n)
                    for j in VALUES_BETWEEN:
                        copy_values(j)
                    tables(b + 1, True)
                    for j in VALUES_BY_TRIAL.values():
                        copy_values(j)
                    for j, (lo, n) in enumerate(KEYS):
                        a.wait_ge(score_done.sem, score_done.at(b, j + 1))
                        if j >= 2:
                            a.wait_ge(pv_done.sem, pv_done.at(b, j - 1))
                        both = 2 * (j % 2)
                        a.activation(prob[0:n, j % 2, :, :],
                                                  big_ps[0:n, both:both + 2, :].rearrange("p c (i k) -> p (c i) k", i=4),
                                                  ACT.Exp).then_inc(prob_done.sem, 1)
                        if j == 3:
                            N.scalar(a, b + 1)
                    for m in range(2):
                        a.wait_ge(attn_turned.sem, attn_turned.at(b, m + 1))
                        a.copy(attnT[:, 4 * m:4 * m + 4, :],
                                             turned_ps[m].rearrange("p (i k) -> p i k", i=4)).then_inc(attnT_done.sem, 1)

            @block.tensor
            def _(pe):
                pe.wait_ge(loaded.sem, loaded.at(0, LOADS))
                pe.wait_ge(sel_set.sem, sel_set.at(0, 2))
                pe.wait_ge(ones_set.sem, ones_set.at(0, 2))

                def unit(b, n):
                    if n >= 3:
                        pe.wait_ge(normed_done.sem, normed_done.at(b, n - 2))
                    if n < K_UNITS:
                        g, (lo, hi) = n // len(COLS), COLS[n % len(COLS)]
                        if n == len(COLS) - 1:
                            pe.wait_ge(tail_done.sem, tail_done.at(b))
                        for m in range(CH):
                            mm = pe.matmul(big_ps[:, n % 3, 0:hi - lo], wk[:, m, g * D:(g + 1) * D], ctxT[:, m, lo:hi],
                                           start=(m == 0), stop=(m == CH - 1))
                    else:
                        for h in range(QH):
                            head = (n - K_UNITS) * QH + h
                            for m in range(CH):
                                mm = pe.matmul(big_ps[:, n % 3, h * SEQ:(h + 1) * SEQ],
                                               wq[:, m, head * D:(head + 1) * D], N.xnT[:, m, :],
                                               start=(m == 0), stop=(m == CH - 1))
                    mm.then_inc(unit_done.sem, 1)

                pe.wait_ge(ctx_loaded.sem, ctx_loaded.at(0))
                unit(0, 0)
                unit(0, 1)
                N.tensor(pe, 0, K.ident)
                with pe.Fori(0, BATCH) as b:
                    def square_sums(n):
                        width = unit_views(n)[0]
                        sums = big_ps[:, 3, 0:width] if n % 2 == 0 else pv_ps[:, 2, 0:width]
                        pe.wait_ge(square_done.sem, square_done.at(b, n + 1))
                        if n >= 2:
                            pe.wait_ge(log_done.sem, log_done.at(b, n - 1))
                        pe.matmul(sums, K.ones[:, :], square[:, n % 2, 0:width], start=True, stop=True).then_inc(ss_done.sem, 1)

                    def values(j):
                        lo, n = KEYS[j]
                        if j >= 2:
                            pe.wait_ge(v_copied.sem, v_copied.at(b, j - 1))
                        for m in range(CH):
                            mm = pe.matmul(pv_ps[0:n, j % 2, :], ctxT[:, m, lo:lo + n], wv[:, m, :],
                                           start=(m == 0), stop=(m == CH - 1))
                        mm.then_inc(v_done.sem, 1)

                    for n in range(UNITS):
                        if 2 <= n + 1 < UNITS:
                            unit(b, n + 1)
                        if n in VALUES_BY_UNIT:
                            values(VALUES_BY_UNIT[n])
                        square_sums(n)
                    for j in VALUES_BETWEEN:
                        values(j)
                    pe.wait_ge(low_done.sem, low_done.at(b, UNITS))
                    for i in range(PAIRS):
                        for c, (lo, hi) in enumerate(COLS):
                            m = i * len(COLS) + c
                            if m >= 4:
                                pe.wait_ge(peak_done.sem, peak_done.at(b, m - 3))
                            pe.matmul(big_ps[:, m % 4, 0:hi - lo], q_low[:, 2 * i:2 * i + 2, :],
                                                    k_low[:, i // 2, lo:hi], start=True, stop=True).then_inc(trial_done.sem, 1)
                            if m in VALUES_BY_TRIAL:
                                values(VALUES_BY_TRIAL[m])
                    pe.wait_ge(neg_peak_done.sem, neg_peak_done.at(b))
                    pe.transpose(misc_ps[:, 0:P], neg_peak[:, :], K.ident[:, :]).then_inc(peak_turned.sem, 1)
                    pe.wait_ge(peak_rows_done.sem, peak_rows_done.at(b))

                    def scores(j):
                        lo, n = KEYS[j]
                        if j >= 2:
                            pe.wait_ge(prob_done.sem, prob_done.at(b, j - 1))
                        for g in range(KV):
                            bank = big_ps[0:n, 2 * (j % 2) + g // 2, :]
                            pe.matmul(bank[:, g % 2 * 256:g % 2 * 256 + 256], k_sb[:, g, lo:lo + n],
                                      q_sb[:, 4 * g:4 * g + 4, :], start=(g % 2 == 0), stop=False, skip_group_check=True)
                            for i in range(2 * g, 2 * g + 2):
                                mm = pe.matmul(bank[:, i % 4 * P:(i % 4 + 1) * P], sel[:, i, 0:n], peak_rows[:, :],
                                               start=False, stop=(i % 4 == 3), skip_group_check=True)
                        mm.then_inc(score_done.sem, 1)

                    def weigh(j):
                        lo, n = KEYS[j]
                        pe.wait_ge(prob_done.sem, prob_done.at(b, j + 1))
                        for i in range(PAIRS):
                            mm = pe.matmul(pv_ps[:, i // 3, i % 3 * 129:i % 3 * 129 + 129], prob[0:n, j % 2, i, :],
                                           v_sb[0:n, j, i // 2, :], start=(j == 0 and i % 3 == 0),
                                           stop=(j == len(KEYS) - 1), skip_group_check=True)
                        mm.then_inc(pv_done.sem, 1)

                    scores(0)
                    for j in range(len(KEYS)):
                        if j + 1 < len(KEYS):
                            scores(j + 1)
                        weigh(j)
                        if j == 6:
                            N.tensor(pe, b + 1, K.ident)
                    pe.wait_ge(ctx_loaded.sem, ctx_loaded.at(b + 1))
                    unit(b + 1, 0)
                    pe.wait_ge(attn_done.sem, attn_done.at(b))
                    for m in range(2):
                        for i in range(4):
                            turn = pe.transpose(turned_ps[m][:, i * P:(i + 1) * P], attn[:, 4 * m + i, :], K.ident[:, :])
                        turn.then_inc(attn_turned.sem, 1)
                    unit(b + 1, 1)
                    pe.wait_ge(attnT_done.sem, attnT_done.at(b, 2))
                    for h in range(H):
                        mm = pe.matmul(misc_ps[0:SEQ, 256:512], attnT[:, h // 2, h % 2 * SEQ:(h % 2 + 1) * SEQ],
                                       wo[:, h, :], start=(h == 0), stop=(h == H - 1))
                    mm.then_inc(out_done.sem, 1)

            @block.vector
            def _(v):
                def angle_step(t, k):
                    if k == 1:
                        v.wait_ge(pos_loaded.sem, pos_loaded.at(t, 2))
                        step = v.tensor_scalar(angle[:, :], pos[:, :], inv_freq[:, 0:1], None, ALU.mult)
                    else:
                        v.wait_ge(angle_steps.sem, angle_steps.at(t, k - 1))
                    if k == 2:
                        step = v.tensor_scalar(turns[:, :], angle[:, :], float(1 / (2 * np.pi)), ROUND, ALU.mult, ALU.add)
                    if k == 3:
                        step = v.tensor_scalar(turns[:, :], turns[:, :], ROUND, None, ALU.subtract)
                    if k == 4:
                        step = v.scalar_tensor_tensor(angle[:, :], turns[:, :], -TWO_PI_HIGH, angle[:, :], ALU.mult, ALU.add)
                    if k == 5:
                        step = v.scalar_tensor_tensor(angle[:, :], turns[:, :], -TWO_PI_LOW, angle[:, :], ALU.mult, ALU.add)
                    if k == 6:
                        step = v.tensor_scalar(angle[:, :], angle[:, :], PI_BELOW, -PI_BELOW, ALU.min, ALU.max)
                    step.then_inc(angle_steps.sem, 1)

                def normalise(t):
                    N.vector(v, t)
                    v.wait_ge(N.xnT_done.sem, N.xnT_done.at(t))
                    v.tensor_copy(ctxT[:, :, CTX:ALL], N.xnT[:, :, :]).then_inc(tail_done.sem, 1)

                def low_copy(b, n):
                    width, which, view, table, exact, low = unit_views(n)
                    v.wait_ge(rope_done.sem, rope_done.at(b, n + 1))
                    v.tensor_copy(low, exact).then_inc(low_done.sem, 1)

                N.setup_vector(v)
                v.memset(eps[:, :], 1e-6).then_inc(consts_set.sem, 1)
                v.memset(half_pi[:, :], float(np.pi / 2)).then_inc(consts_set.sem, 1)
                y_done.open(v)
                v.wait_ge(loaded.sem, loaded.at(0, LOADS))
                v.wait_ge(ones_set.sem, ones_set.at(0, 2))
                v.tensor_scalar(norm_w[:, 1:2], norm_w[:, 1:2], float(D) ** -0.5, None, ALU.mult).then_inc(consts_set.sem, 1)
                v.memset(inv[:, :], 0.0).then_inc(consts_set.sem, 1)
                v.wait_ge(consts_set.sem, consts_set.at(0, 4))
                for k in range(1, 7):
                    angle_step(0, k)
                normalise(0)
                with v.Fori(0, BATCH) as b:
                    for n in range(UNITS):
                        width, which, view, table, exact, low = unit_views(n)
                        v.wait_ge(rstd_done.sem, rstd_done.at(b, n + 1))
                        if n >= 2:
                            v.wait_ge(by_cos_done.sem, by_cos_done.at(b, n - 1))
                        now = normed[:, n % 2, :]
                        v.scalar_tensor_tensor(now[:, 0:width], big_ps[:, n % 3, 0:width],
                                                              norm_w[:, which:which + 1], rstd[:, n % 2, 0:width],
                                                              ALU.mult, ALU.mult).then_inc(normed_done.sem, 1)
                        v.wait_ge(normed_done.sem, normed_done.at(b, n + 1))
                        if n >= 2:
                            v.wait_ge(rope_done.sem, rope_done.at(b, n - 1))
                        for half in range(2):
                            src = slice(half * HALF, (half + 1) * HALF)
                            dst = slice((1 - half) * HALF, (2 - half) * HALF)
                            last = v.tensor_tensor(view(by_sin[:, n % 2, :])[dst], view(now)[src], table(sin[src, :]),
                                                   ALU.mult)
                        last.then_inc(by_sin_done.sem, 1)
                        if n >= 1:
                            low_copy(b, n - 1)
                        if n == 2:
                            v.wait_ge(table_done.sem, table_done.at(b, 3))
                        if 3 <= n < 9:
                            angle_step(b + 1, n - 2)
                    low_copy(b, UNITS - 1)
                    for m in range(PAIRS * len(COLS)):
                        i, c = m // len(COLS), m % len(COLS)
                        v.wait_ge(trial_done.sem, trial_done.at(b, m + 1))
                        v.tensor_reduce(peaks[:, c, i:i + 1], big_ps[:, m % 4, 0:COLS[c][1] - COLS[c][0]],
                                                     AX.X, ALU.max).then_inc(peak_done.sem, 1)
                    v.wait_ge(peak_done.sem, peak_done.at(b, PAIRS * len(COLS)))
                    v.tensor_reduce(neg_peak[:, 0:PAIRS], peaks[:, :, :].rearrange("p c i -> p i c"),
                                                     AX.X, ALU.max, negate=True).then_inc(neg_peak_done.sem, 1)
                    v.wait_ge(peak_turned.sem, peak_turned.at(b))
                    v.tensor_copy(peak_rows[:, :], misc_ps[:, 0:P]).then_inc(peak_rows_done.sem, 1)
                    normalise(b + 1)
                    v.wait_ge(pv_done.sem, pv_done.at(b, len(KEYS)))
                    for m in range(3):
                        heads = min(3, PAIRS - 3 * m)
                        last = v.reciprocal(inv[:, 3 * m:3 * m + heads],
                                            pv_ps[:, m, 0:heads * 129].rearrange("p (i d) -> p i d", d=129)[:, :, 128])
                    last.then_inc(inv_done.sem, 1)
                    v.wait_ge(inv_done.sem, inv_done.at(b))
                    for i in range(PAIRS):
                        last = v.tensor_scalar(attn[:, i, :], pv_ps[:, i // 3, i % 3 * 129:i % 3 * 129 + 128],
                                               inv[:, i:i + 1], None, ALU.mult)
                    last.then_inc(attn_done.sem, 1)
                    v.wait_ge(out_done.sem, out_done.at(b))
                    v.wait_ge(stored.sem, stored.before(b))
                    v.wait_ge(residual_loaded.sem, residual_loaded.at(b))
                    v.tensor_tensor(y[:, :], misc_ps[0:SEQ, 256:512], residual[:, :], ALU.add).then_inc(y_done.sem, 1)
        S.clear()




class SelfSoftmax:

    def __init__(self, S, score_ps, turn_ps, scale):
        self.score_ps, self.turn_ps, self.scale = score_ps, turn_ps, scale
        self.mask = S.sb("mask", [P, P])
        self.shifted = S.sb("shifted", [P, 4, 4, P])
        self.neg_peak = S.sb("neg_peak", [P, 16])
        self.prob = S.sb("prob", [P, 4, 4, P])
        self.total = S.sb("total", [P, 16])
        self.inv = S.sb("inv", [P, 16])
        self.probT = S.sb("probT", [P, 16, P])
        self.mask_set = S.sig("mask_set", per=3)
        self.scores_done = S.sig("scores_done", per=4)
        self.masked_done = S.sig("masked_done", per=4)
        self.peak_done = S.sig("peak_done", per=4)
        self.shifted_done = S.sig("shifted_done", per=4)
        self.exp_done = S.sig("exp_done", per=4)
        self.total_done = S.sig("total_done", per=4)
        self.inv_done = S.sig("inv_done", per=4)
        self.prob_done = S.sig("prob_done", per=4)
        self.prob_turned = S.sig("prob_turned", per=4)
        self.probT_done = S.sig("probT_done", per=4)

    def setup_gpsimd(self, g):
        g.memset(self.mask[:, :], 0.0).then_inc(self.mask_set.sem, 1)
        g.wait_ge(self.mask_set.sem, self.mask_set.at(0, 1))
        g.affine_select(out=self.mask[:, :], in_=self.mask[:, :], compare_op=ALU.is_ge, fill=-1e30,
                                         base=0, pattern=[[-1, P]], channel_multiplier=1).then_inc(self.mask_set.sem, 1)
        g.wait_ge(self.mask_set.sem, self.mask_set.at(0, 2))
        g.memset(self.mask[SEQ:P, 0:SEQ], -1e30).then_inc(self.mask_set.sem, 1)
        g.wait_ge(self.mask_set.sem, self.mask_set.at(0, 3))

    def _four(self, ap, n):
        return ap[:, 4 * n:4 * n + 4].unsqueeze(2).broadcast_to([P, 4, P])

    def vector(self, v, t):
        for n in range(4):
            v.wait_ge(self.scores_done.sem, self.scores_done.at(t, n + 1))
            v.scalar_tensor_tensor(
                self.shifted[:, n, :, :], self.score_ps[:, n, :].rearrange("p (h k) -> p h k", h=4), self.scale,
                self.mask[:, :].unsqueeze(1).broadcast_to([P, 4, P]), ALU.mult, ALU.add).then_inc(self.masked_done.sem, 1)
            v.wait_ge(self.masked_done.sem, self.masked_done.at(t, n + 1))
            v.tensor_reduce(self.neg_peak[:, 4 * n:4 * n + 4], self.shifted[:, n, :, :], AX.X,
                                              ALU.max, negate=True).then_inc(self.peak_done.sem, 1)
        for n in range(4):
            v.wait_ge(self.exp_done.sem, self.exp_done.at(t, n + 1))
            v.tensor_reduce(self.total[:, 4 * n:4 * n + 4], self.prob[:, n, :, :], AX.X, ALU.add).then_inc(self.total_done.sem, 1)
            v.wait_ge(self.total_done.sem, self.total_done.at(t, n + 1))
            v.reciprocal(self.inv[:, 4 * n:4 * n + 4], self.total[:, 4 * n:4 * n + 4]).then_inc(self.inv_done.sem, 1)

    def gpsimd(self, g, t):
        for n in range(4):
            g.wait_ge(self.peak_done.sem, self.peak_done.at(t, n + 1))
            g.tensor_tensor(self.shifted[:, n, :, :], self.shifted[:, n, :, :],
                                                 self._four(self.neg_peak, n), ALU.add).then_inc(self.shifted_done.sem, 1)
        for n in range(4):
            g.wait_ge(self.inv_done.sem, self.inv_done.at(t, n + 1))
            g.tensor_tensor(self.prob[:, n, :, :], self.prob[:, n, :, :], self._four(self.inv, n),
                                              ALU.mult).then_inc(self.prob_done.sem, 1)

    def scalar(self, a, t):
        for n in range(4):
            a.wait_ge(self.shifted_done.sem, self.shifted_done.at(t, n + 1))
            a.activation(self.prob[:, n, :, :], self.shifted[:, n, :, :], ACT.Exp).then_inc(self.exp_done.sem, 1)
        for n in range(4):
            a.wait_ge(self.prob_turned.sem, self.prob_turned.at(t, n + 1))
            a.copy(self.probT[:, 4 * n:4 * n + 4, :],
                                      self.turn_ps[:, n % 2, :].rearrange("p (h k) -> p h k", h=4)).then_inc(self.probT_done.sem, 1)

    def tensor(self, pe, t, ident):
        for n in range(4):
            pe.wait_ge(self.prob_done.sem, self.prob_done.at(t, n + 1))
            if n >= 2:
                pe.wait_ge(self.probT_done.sem, self.probT_done.at(t, n - 1))
            for h in range(4):
                turn = pe.transpose(self.turn_ps[:, n % 2, h * P:(h + 1) * P], self.prob[:, n, h, :], ident[:, :])
            turn.then_inc(self.prob_turned.sem, 1)


def gated_attention(nc, K, x_in, x_out, A):
    H, KV, D = 16, 4, 128
    HALF = D // 2
    PAIRS = H // 2 + KV // 2
    UNITS = PAIRS // 2
    with ExitStack() as ctx:
        S = Space(nc, ctx, "gated")
        wqk = S.sb("wqk", [P, CH, (H + KV) * D])
        wv = S.sb("wv", [P, CH, KV * D])
        wg = S.sb("wg", [P, CH, H * D])
        wo = S.sb("wo", [P, H, DIM])
        affine = S.sb("affine", [P, 2, 2, 2])
        cos = S.sb("cos", [P, P])
        sin = S.sb("sin", [P, P])
        eps = S.sb("eps", [P, 1])
        raw = S.sb("raw", [P, UNITS, 512])
        head_stats = S.sb("head_stats", [P, 2 * PAIRS, 6])
        head_mv = S.sb("head_mv", [P, 2 * PAIRS, 2])
        head_log = S.sb("head_log", [P, 2 * PAIRS])
        head_rstd = S.sb("head_rstd", [P, 2 * PAIRS])
        turned = S.sb("turned", [P, 2, PAIRS, P])
        rope = S.sb("rope", [P, 2, PAIRS, P])
        by_cos = S.sb("by_cos", [P, 2, PAIRS, P])
        by_sin = S.sb("by_sin", [P, 2, PAIRS, P])
        v_sb = S.sb("v", [P, KV * D])
        gate = S.sb("gate", [P, H, P])
        gated = S.sb("gated", [P, H, P])
        y = S.sb("y", [P, DIM])
        proj_ps = S.ps("proj_ps", [P, 2, 512])
        turn_ps = S.ps("turn_ps", [P, 2, 512])
        score_ps = S.ps("score_ps", [P, 4, 512])

        N = Norm(S, P, turn_ps[:, 0, 0:DIM].rearrange("p (c k) -> p c k", c=CH))
        soft = SelfSoftmax(S, score_ps, turn_ps, float(D) ** -0.5)
        small_loaded = S.dma("small_loaded", per=12)
        wqk_loaded = S.dma("wqk_loaded", per=1)
        wvg_loaded = S.dma("wvg_loaded", per=2)
        wo_loaded = S.dma("wo_loaded", per=1)
        eps_set = S.sig("eps_set")
        projected = S.sig("projected", per=10)
        raw_done = S.sig("raw_done", per=UNITS)
        head_stats_done = S.sig("head_stats_done", per=UNITS)
        head_mv_done = S.sig("head_mv_done")
        head_log_done = S.sig("head_log_done")
        head_rstd_done = S.sig("head_rstd_done")
        normed_done = S.sig("normed_done", per=UNITS)
        qk_turned = S.sig("qk_turned", per=UNITS)
        affine_done = S.sig("affine_done", per=UNITS)
        cos_done = S.sig("cos_done")
        sin_done = S.sig("sin_done")
        rope_done = S.sig("rope_done", per=2)
        v_done = S.sig("v_done")
        gate_done = S.sig("gate_done", per=4)
        pv_done = S.sig("pv_done", per=4)
        gated_done = S.sig("gated_done", per=4)
        out_done = S.sig("out_done")
        y_done = S.sig("y_done", credit=1)
        stored = S.dma("stored", credit=1)

        with nc.Block() as block:
            @block.sync
            def _(sp):
                stored.open(sp)
                sp.dma_start(N.x[:, :], x_in[0]).then_inc(N.x_loaded.sem, 16)
                for half in range(2):
                    rows = slice(half * HALF, (half + 1) * HALF)
                    for n, name in enumerate(("q_norm_w", "q_norm_b", "k_norm_w", "k_norm_b")):
                        sp.dma_start(affine[rows, n // 2, n % 2, :], A[f"L0_attn_{name}"]).then_inc(small_loaded.sem, 16)
                    sp.dma_start(cos[rows, :], A["gated_cos"]).then_inc(small_loaded.sem, 16)
                    sp.dma_start(sin[rows, :], A["gated_sin"]).then_inc(small_loaded.sem, 16)
                sp.dma_start(wqk[:, :, :], A["L0_attn_wqk"].rearrange("(c p) n -> p c n", p=P)).then_inc(wqk_loaded.sem, 16)
                sp.dma_start(wv[:, :, :], A["L0_attn_wv"].rearrange("(c p) n -> p c n", p=P)).then_inc(wvg_loaded.sem, 16)
                sp.dma_start(wg[:, :, :], A["L0_attn_wg"].rearrange("(c p) n -> p c n", p=P)).then_inc(wvg_loaded.sem, 16)
                sp.dma_start(wo[:, :, :], A["L0_attn_w_o"].rearrange("(h p) n -> p h n", p=P)).then_inc(wo_loaded.sem, 16)
                with sp.Fori(0, TILES - 1) as t:
                    sp.wait_ge(y_done.sem, y_done.at(t))
                    sp.dma_start(x_out[t], y[:, :]).then_inc(stored.sem, 16)
                    sp.dma_start(N.x[:, :], x_in[t + 1]).then_inc(N.x_loaded.sem, 16)
                sp.wait_ge(y_done.sem, y_done.at(TILES - 1))
                sp.dma_start(x_out[TILES - 1], y[:, :]).then_inc(stored.sem, 16)
                sp.wait_ge(stored.sem, stored.before(TILES))

            @block.gpsimd
            def _(g):
                soft.setup_gpsimd(g)
                g.wait_ge(small_loaded.sem, small_loaded.at(0, 12))
                with g.Fori(0, TILES) as t:
                    g.wait_ge(affine_done.sem, affine_done.at(t, UNITS))
                    wide_sin = sin[:, :].unsqueeze(1).broadcast_to([P, 2 * PAIRS, P])
                    g.tensor_tensor(by_sin[:, :, :, :].rearrange("p a r k -> p (a r) k"),
                                                turned[:, :, :, :].rearrange("p a r k -> p (a r) k"), wide_sin, ALU.mult).then_inc(sin_done.sem, 1)
                    g.wait_ge(cos_done.sem, cos_done.at(t))
                    g.wait_ge(sin_done.sem, sin_done.at(t))
                    g.tensor_tensor(rope[:, 1, :, :], by_cos[:, 1, :, :], by_sin[:, 0, :, :], ALU.add).then_inc(rope_done.sem, 1)
                    soft.gpsimd(g, t)

            @block.scalar
            def _(a):
                a.preload_act_table_set("natural_log_exp_and_others")
                a.wait_ge(N.eps_set.sem, N.eps_set.at(0))
                a.wait_ge(eps_set.sem, eps_set.at(0))
                a.wait_ge(small_loaded.sem, small_loaded.at(0, 12))
                with a.Fori(0, TILES) as t:
                    a.preload_act_table_set("natural_log_exp_and_others")
                    N.scalar(a, t)
                    for n in range(UNITS):
                        a.wait_ge(projected.sem, projected.at(t, n + 1))
                        a.copy(raw[:, n, :], proj_ps[:, n % 2, :]).then_inc(raw_done.sem, 1)
                    a.wait_ge(head_mv_done.sem, head_mv_done.at(t))
                    a.activation(head_log[:, :], head_mv[:, :, 1], ACT.Ln, bias=eps[:, 0:1]).then_inc(head_log_done.sem, 1)
                    a.wait_ge(head_log_done.sem, head_log_done.at(t))
                    a.activation(head_rstd[:, :], head_log[:, :], ACT.Exp, scale=-0.5).then_inc(head_rstd_done.sem, 1)
                    a.wait_ge(projected.sem, projected.at(t, UNITS + 1))
                    a.copy(v_sb[:, :], proj_ps[:, UNITS % 2, :]).then_inc(v_done.sem, 1)
                    for n in range(UNITS):
                        which = 0 if n < UNITS - 1 else 1
                        a.wait_ge(qk_turned.sem, qk_turned.at(t, n + 1))
                        for part in range(2):
                            last = a.activation(
                                turned[:, part, 2 * n:2 * n + 2, :],
                                turn_ps[:, n % 2, :].rearrange("p (r a k) -> p r a k", r=2, a=2)[:, :, part, :],
                                ACT.Identity, bias=affine[:, which, 1, part:part + 1],
                                scale=affine[:, which, 0, part:part + 1])
                        last.then_inc(affine_done.sem, 1)
                    for n in range(4):
                        a.wait_ge(projected.sem, projected.at(t, UNITS + 2 + n))
                        a.activation(gate[:, 4 * n:4 * n + 4, :], proj_ps[:, n % 2, :], ACT.Sigmoid).then_inc(gate_done.sem, 1)
                    soft.scalar(a, t)

            @block.tensor
            def _(pe):
                pe.wait_ge(wqk_loaded.sem, wqk_loaded.at(0))
                pe.wait_ge(wvg_loaded.sem, wvg_loaded.at(0, 2))
                pe.wait_ge(wo_loaded.sem, wo_loaded.at(0))
                with pe.Fori(0, TILES) as t:
                    N.tensor(pe, t, K.ident)
                    pe.wait_ge(N.xnT_done.sem, N.xnT_done.at(t))
                    for n in range(UNITS + 1):
                        if n >= 2:
                            pe.wait_ge(raw_done.sem, raw_done.at(t, n - 1))
                        for c in range(CH):
                            w = wqk[:, c, n * 512:(n + 1) * 512] if n < UNITS else wv[:, c, :]
                            mm = pe.matmul(proj_ps[:, n % 2, :], N.xnT[:, c, :], w, start=(c == 0), stop=(c == 1))
                        mm.then_inc(projected.sem, 1)
                    for n in range(UNITS):
                        pe.wait_ge(normed_done.sem, normed_done.at(t, n + 1))
                        if n >= 2:
                            pe.wait_ge(affine_done.sem, affine_done.at(t, n - 1))
                        for m in range(4):
                            turn = pe.transpose(turn_ps[:, n % 2, m * P:(m + 1) * P], raw[:, n, m * P:(m + 1) * P],
                                                K.ident[:, :])
                        turn.then_inc(qk_turned.sem, 1)
                    for n in range(4):
                        if n == 0:
                            pe.wait_ge(raw_done.sem, raw_done.at(t, UNITS))
                        if n == 1:
                            pe.wait_ge(v_done.sem, v_done.at(t))
                        if n >= 2:
                            pe.wait_ge(gate_done.sem, gate_done.at(t, n - 1))
                        for h in range(4):
                            for c in range(CH):
                                mm = pe.matmul(proj_ps[:, n % 2, h * P:(h + 1) * P],
                                               wg[:, c, (4 * n + h) * P:(4 * n + h + 1) * P], N.xnT[:, c, :],
                                               start=(c == 0), stop=(c == 1))
                        mm.then_inc(projected.sem, 1)
                    pe.wait_ge(rope_done.sem, rope_done.at(t, 2))
                    for n in range(4):
                        half, u = n // 2, n % 2
                        rows = slice(half * HALF, (half + 1) * HALF)
                        for j in range(4):
                            for part in range(2):
                                mm = pe.matmul(score_ps[:, n, j * P:(j + 1) * P], rope[rows, part, 4 * u + j, :],
                                               rope[rows, part, H // 2 + u, :], start=(part == 0), stop=(part == 1))
                        mm.then_inc(soft.scores_done.sem, 1)
                    soft.tensor(pe, t, K.ident)
                    pe.wait_ge(v_done.sem, v_done.at(t))
                    for n in range(4):
                        place = (n % 2) * 2 + n // 2
                        pe.wait_ge(soft.probT_done.sem, soft.probT_done.at(t, place + 1))
                        pe.matmul(score_ps[:, n, :], v_sb[:, n * P:(n + 1) * P],
                                             soft.probT[:, 4 * place:4 * place + 4, :], start=True, stop=True).then_inc(pv_done.sem, 1)
                    pe.wait_ge(soft.probT_done.sem, soft.probT_done.at(t, 4))
                    for h in range(H):
                        if h % 4 == 0:
                            pe.wait_ge(gated_done.sem, gated_done.at(t, h // 4 + 1))
                        mm = pe.matmul(turn_ps[:, 0, 0:DIM], gated[:, h, :], wo[:, h, :], start=(h == 0), stop=(h == H - 1))
                    mm.then_inc(out_done.sem, 1)

            @block.vector
            def _(v):
                N.setup_vector(v)
                v.memset(eps[:, :], 1e-6).then_inc(eps_set.sem, 1)
                y_done.open(v)
                v.wait_ge(soft.mask_set.sem, soft.mask_set.at(0, 3))
                v.wait_ge(small_loaded.sem, small_loaded.at(0, 12))
                with v.Fori(0, TILES) as t:
                    N.vector(v, t)
                    for n in range(UNITS):
                        v.wait_ge(raw_done.sem, raw_done.at(t, n + 1))
                        bank = raw[:, n, :].rearrange("p (r a h d) -> p r a h d", r=2, a=2, h=2)
                        for r in range(2):
                            for half in range(2):
                                last = v.bn_stats(head_stats[:, 4 * n + 2 * r + half, :], bank[:, r, :, half, :])
                        last.then_inc(head_stats_done.sem, 1)
                    v.wait_ge(head_stats_done.sem, head_stats_done.at(t, UNITS))
                    v.sem_inc(N.paused.sem, 1)
                    for h in range(2 * PAIRS):
                        last = v.bn_aggr(head_mv[:, h, :], head_stats[:, h, :])
                    last.then_inc(head_mv_done.sem, 1)
                    v.wait_ge(head_mv_done.sem, head_mv_done.at(t))
                    v.wait_ge(head_rstd_done.sem, head_rstd_done.at(t))
                    for n in range(UNITS):
                        v.wait_ge(raw_done.sem, raw_done.at(t, n + 1))
                        view = raw[:, n, :].rearrange("p (r a h d) -> p r a h d", r=2, a=2, h=2)
                        for r in range(2):
                            for half in range(2):
                                h = 4 * n + 2 * r + half
                                last = v.tensor_scalar(view[:, r, :, half, :], view[:, r, :, half, :],
                                                       head_mv[:, h, 0:1], head_rstd[:, h:h + 1],
                                                       ALU.subtract, ALU.mult)
                        last.then_inc(normed_done.sem, 1)
                    v.wait_ge(affine_done.sem, affine_done.at(t, UNITS))
                    wide_cos = cos[:, :].unsqueeze(1).broadcast_to([P, 2 * PAIRS, P])
                    v.tensor_tensor(by_cos[:, :, :, :].rearrange("p a r k -> p (a r) k"),
                                                turned[:, :, :, :].rearrange("p a r k -> p (a r) k"), wide_cos, ALU.mult).then_inc(cos_done.sem, 1)
                    v.wait_ge(cos_done.sem, cos_done.at(t))
                    v.wait_ge(sin_done.sem, sin_done.at(t))
                    v.tensor_tensor(rope[:, 0, :, :], by_cos[:, 0, :, :], by_sin[:, 1, :, :], ALU.subtract).then_inc(rope_done.sem, 1)
                    soft.vector(v, t)
                    v.wait_ge(gate_done.sem, gate_done.at(t, 4))
                    for n in range(4):
                        v.wait_ge(pv_done.sem, pv_done.at(t, n + 1))
                        v.tensor_tensor(gated[:, 4 * n:4 * n + 4, :],
                                                      score_ps[:, n, :].rearrange("p (h k) -> p h k", h=4),
                                                      gate[:, 4 * n:4 * n + 4, :], ALU.mult).then_inc(gated_done.sem, 1)
                    v.wait_ge(out_done.sem, out_done.at(t))
                    v.wait_ge(stored.sem, stored.before(t))
                    v.tensor_tensor(y[:, :], turn_ps[:, 0, 0:DIM], N.x[:, :], ALU.add).then_inc(y_done.sem, 1)
        S.clear()


def rotary_attention(nc, K, x_in, x_out, A):
    H, D = 16, 16
    G = 2 * H
    with ExitStack() as ctx:
        S = Space(nc, ctx, "rotary")
        wq = S.sb("wq", [P, CH, DIM])
        wkv = S.sb("wkv", [P, CH, 2 * DIM])
        wo = S.sb("wo", [P, CH, DIM])
        bq = S.sb("bq", [1, DIM])
        bkv = S.sb("bkv", [1, 2 * DIM])
        bo = S.sb("bo", [1, DIM])
        gains = S.sb("gains", [P, 4, CH])
        head_g = S.sb("head_g", [P, D])
        head_b = S.sb("head_b", [P, D])
        cos = S.sb("cos", [P, D // 2])
        sin = S.sb("sin", [P, D // 2])
        parity = S.sb("parity", [P, 2])
        eps = S.sb("eps", [P, 1])
        stats2 = S.sb("stats2", [P, 6])
        mv2 = S.sb("mv2", [P, 2])
        log2 = S.sb("log2", [P, 2])
        power2 = S.sb("power2", [P, 2])
        square = S.sb("square", [P, 1])
        size = S.sb("size", [P, 1])
        xn2 = S.sb("xn2", [P, DIM])
        xqT = S.sb("xqT", [P, CH, P])
        xkvT = S.sb("xkvT", [P, CH, P])
        raw = S.sb("raw", [P, G, D])
        v_sb = S.sb("v", [P, DIM])
        mcos = S.sb("mcos", [P, D // 2])
        msin = S.sb("msin", [P, D // 2])
        t_ac = S.sb("t_ac", [P, G, D // 2])
        t_bs = S.sb("t_bs", [P, G, D // 2])
        t_as = S.sb("t_as", [P, G, D // 2])
        t_bc = S.sb("t_bc", [P, G, D // 2])
        rot = S.sb("rot", [P, G, D])
        head_sum = S.sb("head_sum", [P, G])
        head_mean = S.sb("head_mean", [P, G])
        squares = S.sb("squares", [P, G, D])
        head_ss = S.sb("head_ss", [P, G])
        head_log = S.sb("head_log", [P, G])
        head_rstd = S.sb("head_rstd", [P, G])
        q_par = S.sb("q_par", [P, 2, CH, P])
        kT = S.sb("kT", [P, CH, P])
        attn = S.sb("attn", [P, DIM])
        attnT = S.sb("attnT", [P, CH, P])
        y = S.sb("y", [P, DIM])
        proj_ps = S.ps("proj_ps", [P, 2, 512])
        turn_ps = S.ps("turn_ps", [P, 2, 512])
        score_ps = S.ps("score_ps", [P, 4, 512])

        two = lambda ap: ap.rearrange("p (c k) -> p c k", c=CH)
        N = Norm(S, P, two(turn_ps[:, 0, 0:DIM]))
        soft = SelfSoftmax(S, score_ps, turn_ps, float(D) ** -0.5)
        loaded = S.dma("loaded", per=14)
        eps_set = S.sig("eps_set")
        parity_set = S.sig("parity_set", per=10)
        chain = S.sig("chain", per=15)
        ready2 = S.sig("ready2")
        log2_done = S.sig("log2_done")
        power2_done = S.sig("power2_done")
        xn2_done = S.sig("xn2_done")
        turned2 = S.sig("turned2")
        inputs_done = S.sig("inputs_done", per=4)
        projected = S.sig("projected", per=2)
        raw_done = S.sig("raw_done", per=3)
        ss_done = S.sig("ss_done")
        head_log_done = S.sig("head_log_done")
        head_rstd_done = S.sig("head_rstd_done")
        normed_done = S.sig("normed_done")
        qk_turned = S.sig("qk_turned")
        qk_done = S.sig("qk_done", per=3)
        pv_done = S.sig("pv_done")
        attn_done = S.sig("attn_done")
        attn_turned = S.sig("attn_turned")
        attnT_done = S.sig("attnT_done")
        out_done = S.sig("out_done")
        y_done = S.sig("y_done", credit=1)
        stored = S.dma("stored", credit=1)

        with nc.Block() as block:
            @block.sync
            def _(sp):
                stored.open(sp)
                sp.dma_start(N.x[:, :], x_in[0]).then_inc(N.x_loaded.sem, 16)
                for n, name in enumerate(("qn_g", "qn_b", "kvn_g", "kvn_b")):
                    sp.dma_start(gains[:, n, :], A[f"L1_attn_{name}"]).then_inc(loaded.sem, 16)
                sp.dma_start(head_g[:, :], A["L1_attn_ln_g"].broadcast_to([P, D])).then_inc(loaded.sem, 16)
                sp.dma_start(head_b[:, :], A["L1_attn_ln_b"].broadcast_to([P, D])).then_inc(loaded.sem, 16)
                sp.dma_start(cos[:, :], A["rotary_cos"]).then_inc(loaded.sem, 16)
                sp.dma_start(sin[:, :], A["rotary_sin"]).then_inc(loaded.sem, 16)
                sp.dma_start(wq[:, :, :], A["L1_attn_Wq"].rearrange("(c p) n -> p c n", p=P)).then_inc(loaded.sem, 16)
                sp.dma_start(wkv[:, :, :], A["L1_attn_Wkv"].rearrange("(c p) n -> p c n", p=P)).then_inc(loaded.sem, 16)
                sp.dma_start(wo[:, :, :], A["L1_attn_Wo"].rearrange("(c p) n -> p c n", p=P)).then_inc(loaded.sem, 16)
                sp.dma_start(bq[:, :], A["L1_attn_bq"]).then_inc(loaded.sem, 16)
                sp.dma_start(bkv[:, :], A["L1_attn_bkv"]).then_inc(loaded.sem, 16)
                sp.dma_start(bo[:, :], A["L1_attn_bo"]).then_inc(loaded.sem, 16)
                with sp.Fori(0, TILES - 1) as t:
                    sp.wait_ge(y_done.sem, y_done.at(t))
                    sp.dma_start(x_out[t], y[:, :]).then_inc(stored.sem, 16)
                    sp.dma_start(N.x[:, :], x_in[t + 1]).then_inc(N.x_loaded.sem, 16)
                sp.wait_ge(y_done.sem, y_done.at(TILES - 1))
                sp.dma_start(x_out[TILES - 1], y[:, :]).then_inc(stored.sem, 16)
                sp.wait_ge(stored.sem, stored.before(TILES))

            @block.gpsimd
            def _(g):
                soft.setup_gpsimd(g)
                make_parity(g, parity, parity_set)
                with g.Fori(0, TILES) as t:
                    soft.gpsimd(g, t)

            @block.scalar
            def _(a):
                a.preload_act_table_set("natural_log_exp_and_others")
                a.wait_ge(N.eps_set.sem, N.eps_set.at(0))
                a.wait_ge(eps_set.sem, eps_set.at(0))
                a.wait_ge(loaded.sem, loaded.at(0, 14))
                with a.Fori(0, TILES) as t:
                    a.preload_act_table_set("natural_log_exp_and_others")
                    N.scalar(a, t)
                    a.wait_ge(ready2.sem, ready2.at(t))
                    a.activation(log2[:, :], mv2[:, :], ACT.Ln).then_inc(log2_done.sem, 1)
                    a.wait_ge(log2_done.sem, log2_done.at(t))
                    a.activation(power2[:, 0:1], log2[:, 0:1], ACT.Exp, scale=-0.5)
                    a.activation(power2[:, 1:2], log2[:, 1:2], ACT.Exp, scale=0.5).then_inc(power2_done.sem, 1)
                    a.wait_ge(turned2.sem, turned2.at(t))
                    for n, T in enumerate((xqT, xkvT)):
                        for c in range(CH):
                            a.activation(T[:, c, :], turn_ps[:, 1, c * P:(c + 1) * P], ACT.Identity,
                                                        bias=gains[:, 2 * n + 1, c:c + 1], scale=gains[:, 2 * n, c:c + 1]).then_inc(inputs_done.sem, 1)
                    a.wait_ge(projected.sem, projected.at(t, 1))
                    a.copy(raw[:, 0:H, :], proj_ps[:, 0, 0:DIM].rearrange("p (h d) -> p h d", h=H)).then_inc(raw_done.sem, 1)
                    a.wait_ge(projected.sem, projected.at(t, 2))
                    a.copy(raw[:, H:G, :], proj_ps[:, 1, 0:DIM].rearrange("p (h d) -> p h d", h=H)).then_inc(raw_done.sem, 1)
                    a.copy(v_sb[:, :], proj_ps[:, 1, DIM:2 * DIM]).then_inc(raw_done.sem, 1)
                    a.wait_ge(ss_done.sem, ss_done.at(t))
                    a.activation(head_log[:, :], head_ss[:, :], ACT.Ln, scale=1.0 / D, bias=N.eps[:, 0:1]).then_inc(head_log_done.sem, 1)
                    a.wait_ge(head_log_done.sem, head_log_done.at(t))
                    a.activation(head_rstd[:, :], head_log[:, :], ACT.Exp, scale=-0.5).then_inc(head_rstd_done.sem, 1)
                    soft.scalar(a, t)
                    a.wait_ge(attn_turned.sem, attn_turned.at(t))
                    a.copy(attnT[:, :, :], two(turn_ps[:, 0, 0:DIM])).then_inc(attnT_done.sem, 1)

            @block.tensor
            def _(pe):
                pe.wait_ge(loaded.sem, loaded.at(0, 14))
                with pe.Fori(0, TILES) as t:
                    N.tensor(pe, t, K.ident)
                    pe.wait_ge(xn2_done.sem, xn2_done.at(t))
                    for c in range(CH):
                        turn = pe.transpose(turn_ps[:, 1, c * P:(c + 1) * P], xn2[:, c * P:(c + 1) * P], K.ident[:, :])
                    turn.then_inc(turned2.sem, 1)
                    pe.wait_ge(inputs_done.sem, inputs_done.at(t, 2))
                    for c in range(CH):
                        pe.matmul(proj_ps[:, 0, 0:DIM], xqT[:, c, :], wq[:, c, :], start=(c == 0), stop=False)
                    pe.matmul(proj_ps[:, 0, 0:DIM], K.ones[0:1, :], bq[0:1, :], start=False, stop=True).then_inc(projected.sem, 1)
                    pe.wait_ge(inputs_done.sem, inputs_done.at(t, 4))
                    for c in range(CH):
                        pe.matmul(proj_ps[:, 1, :], xkvT[:, c, :], wkv[:, c, :], start=(c == 0), stop=False)
                    pe.matmul(proj_ps[:, 1, :], K.ones[0:1, :], bkv[0:1, :], start=False, stop=True).then_inc(projected.sem, 1)
                    pe.wait_ge(normed_done.sem, normed_done.at(t))
                    flat = rot[:, :, :].rearrange("p h d -> p (h d)")
                    for m in range(4):
                        turn = pe.transpose(turn_ps[:, 0, m * P:(m + 1) * P], flat[:, m * P:(m + 1) * P], K.ident[:, :])
                    turn.then_inc(qk_turned.sem, 1)
                    pe.wait_ge(qk_done.sem, qk_done.at(t, 3))
                    for n in range(4):
                        rows = slice(32 * n, 32 * n + 32)
                        for c in range(CH):
                            for par in range(2):
                                slot = 2 * c + par
                                mm = pe.matmul(score_ps[:, n, slot * P:(slot + 1) * P], q_par[rows, par, c, :],
                                               kT[rows, c, :], start=True, stop=True)
                        mm.then_inc(soft.scores_done.sem, 1)
                    soft.tensor(pe, t, K.ident)
                    pe.wait_ge(soft.probT_done.sem, soft.probT_done.at(t, 4))
                    pe.wait_ge(raw_done.sem, raw_done.at(t, 3))
                    for h in range(H):
                        place = (h % 8 // 2) * 4 + (h // 8) * 2 + h % 2
                        mm = pe.matmul(proj_ps[:, 0, h * D:(h + 1) * D], soft.probT[:, place, :],
                                       v_sb[:, h * D:(h + 1) * D], start=(h == 0), stop=(h == H - 1), skip_group_check=True)
                    mm.then_inc(pv_done.sem, 1)
                    pe.wait_ge(attn_done.sem, attn_done.at(t))
                    for c in range(CH):
                        turn = pe.transpose(turn_ps[:, 0, c * P:(c + 1) * P], attn[:, c * P:(c + 1) * P], K.ident[:, :])
                    turn.then_inc(attn_turned.sem, 1)
                    pe.wait_ge(attnT_done.sem, attnT_done.at(t))
                    for c in range(CH):
                        pe.matmul(turn_ps[:, 1, 0:DIM], attnT[:, c, :], wo[:, c, :], start=(c == 0), stop=False)
                    pe.matmul(turn_ps[:, 1, 0:DIM], K.ones[0:1, :], bo[0:1, :], start=False, stop=True).then_inc(out_done.sem, 1)

            @block.vector
            def _(v):
                N.setup_vector(v)
                v.memset(eps[:, :], 1e-5).then_inc(eps_set.sem, 1)
                y_done.open(v)
                v.wait_ge(soft.mask_set.sem, soft.mask_set.at(0, 3))
                v.wait_ge(parity_set.sem, parity_set.at(0, 10))
                v.wait_ge(loaded.sem, loaded.at(0, 14))
                with v.Fori(0, TILES) as t:
                    step = [0]

                    def chained(instruction, alone=None):
                        step[0] += 1
                        instruction.then_inc(chain.sem, 1)
                        v.wait_ge(chain.sem, chain.at(t, step[0]))
                        if alone is not None:
                            v.sem_inc(alone.sem, 1)

                    N.vector(v, t)
                    chained(v.bn_stats(stats2[:, :], N.xn[:, :]), alone=N.paused)
                    chained(v.bn_aggr(mv2[:, :], stats2[:, :]))
                    chained(v.tensor_tensor(square[:, :], mv2[:, 0:1], mv2[:, 0:1], ALU.mult))
                    chained(v.tensor_scalar(square[:, :], square[:, :], mv2[:, 1:2], float(DIM), ALU.add, ALU.mult))
                    chained(v.tensor_scalar(xn2[:, :], N.xn[:, :], mv2[:, 0:1], None, ALU.subtract))
                    chained(v.tensor_scalar(size[:, :], mv2[:, 1:2], 1e-5, None, ALU.add))
                    v.tensor_copy(mv2[:, 0:1], size[:, :])
                    v.tensor_scalar(mv2[:, 1:2], square[:, :], 1e-30, None, ALU.max).then_inc(ready2.sem, 1)
                    v.wait_ge(power2_done.sem, power2_done.at(t))
                    v.tensor_scalar(xn2[:, :], xn2[:, :], power2[:, 0:1], None, ALU.mult).then_inc(xn2_done.sem, 1)
                    v.tensor_scalar(mcos[:, :], cos[:, :], power2[:, 1:2], float(D) ** -0.25, ALU.mult, ALU.mult)
                    chained(v.tensor_scalar(msin[:, :], sin[:, :], power2[:, 1:2], float(D) ** -0.25, ALU.mult, ALU.mult))
                    v.wait_ge(raw_done.sem, raw_done.at(t, 2))
                    pairs = raw[:, :, :].rearrange("p h (d e) -> p h d e", e=2)
                    turned = rot[:, :, :].rearrange("p h (d e) -> p h d e", e=2)
                    wc = mcos[:, :].unsqueeze(1).broadcast_to([P, G, D // 2])
                    ws = msin[:, :].unsqueeze(1).broadcast_to([P, G, D // 2])
                    v.tensor_tensor(t_ac[:, :, :], pairs[:, :, :, 0], wc, ALU.mult)
                    v.tensor_tensor(t_bs[:, :, :], pairs[:, :, :, 1], ws, ALU.mult)
                    v.tensor_tensor(t_as[:, :, :], pairs[:, :, :, 0], ws, ALU.mult)
                    chained(v.tensor_tensor(t_bc[:, :, :], pairs[:, :, :, 1], wc, ALU.mult))
                    v.tensor_tensor(turned[:, :, :, 0], t_ac[:, :, :], t_bs[:, :, :], ALU.subtract)
                    chained(v.tensor_tensor(turned[:, :, :, 1], t_as[:, :, :], t_bc[:, :, :], ALU.add))
                    wide = lambda ap: ap.unsqueeze(2).broadcast_to([P, G, D])
                    rows = lambda ap: ap.unsqueeze(1).broadcast_to([P, G, D])
                    chained(v.tensor_reduce(head_sum[:, :], rot[:, :, :], AX.X, ALU.add))
                    chained(v.tensor_scalar(head_mean[:, :], head_sum[:, :], 1.0 / D, None, ALU.mult))
                    chained(v.tensor_tensor(rot[:, :, :], rot[:, :, :], wide(head_mean[:, :]), ALU.subtract))
                    chained(v.tensor_tensor(squares[:, :, :], rot[:, :, :], rot[:, :, :], ALU.mult))
                    v.tensor_reduce(head_ss[:, :], squares[:, :, :], AX.X, ALU.add).then_inc(ss_done.sem, 1)
                    v.wait_ge(head_rstd_done.sem, head_rstd_done.at(t))
                    chained(v.tensor_tensor(rot[:, :, :], rot[:, :, :], wide(head_rstd[:, :]), ALU.mult))
                    chained(v.tensor_tensor(rot[:, :, :], rot[:, :, :], rows(head_g[:, :]), ALU.mult))
                    v.tensor_tensor(rot[:, :, :], rot[:, :, :], rows(head_b[:, :]), ALU.add).then_inc(normed_done.sem, 1)
                    v.wait_ge(qk_turned.sem, qk_turned.at(t))
                    for par in range(2):
                        v.tensor_scalar(q_par[:, par, :, :], two(turn_ps[:, 0, 0:DIM]), parity[:, par:par + 1],
                                                   None, ALU.mult).then_inc(qk_done.sem, 1)
                    v.tensor_copy(kT[:, :, :], two(turn_ps[:, 0, DIM:2 * DIM])).then_inc(qk_done.sem, 1)
                    soft.vector(v, t)
                    v.wait_ge(pv_done.sem, pv_done.at(t))
                    v.tensor_copy(attn[:, :], proj_ps[:, 0, 0:DIM]).then_inc(attn_done.sem, 1)
                    v.wait_ge(out_done.sem, out_done.at(t))
                    v.wait_ge(stored.sem, stored.before(t))
                    v.tensor_tensor(y[:, :], turn_ps[:, 1, 0:DIM], N.x[:, :], ALU.add).then_inc(y_done.sem, 1)
        S.clear()


def make_parity(g, parity, done):
    count = 0
    for column in range(2):
        regions = [(slice(0, P), float(column))] + [(slice(32 * q, 32 * q + 16), 1.0 - column) for q in range(4)]
        for rows, value in regions:
            g.memset(parity[rows, column:column + 1], value).then_inc(done.sem, 1)
            count += 1
            g.wait_ge(done.sem, done.at(0, count))


def rank_mask_vector(v, t, S):
    a = S.score[:, :]
    own = a.unsqueeze(2).broadcast_to([P, 8, 8])
    other = a.unsqueeze(1).broadcast_to([P, 8, 8])
    v.tensor_tensor(S.greater[:, :, :], other, own, ALU.is_gt).then_inc(S.greater_done.sem, 1)
    v.tensor_tensor(S.equal[:, :, :], other, own, ALU.is_equal).then_inc(S.equal_done.sem, 1)
    v.wait_ge(S.equal_done.sem, S.equal_done.at(t))
    v.tensor_tensor(S.tie[:, :, :], S.equal[:, :, :], S.lower[:, :, :], ALU.mult).then_inc(S.tie_done.sem, 1)
    v.wait_ge(S.tie_done.sem, S.tie_done.at(t))
    v.wait_ge(S.greater_done.sem, S.greater_done.at(t))
    v.tensor_tensor(S.beats[:, :, :], S.greater[:, :, :], S.tie[:, :, :], ALU.add).then_inc(S.beats_done.sem, 1)
    v.wait_ge(S.beats_done.sem, S.beats_done.at(t))
    v.tensor_reduce(S.rank[:, :], S.beats[:, :, :], AX.X, ALU.add).then_inc(S.rank_done.sem, 1)
    v.wait_ge(S.rank_done.sem, S.rank_done.at(t))


def rank_space(S):
    S.score = S.sb("score", [P, 8])
    S.greater = S.sb("greater", [P, 8, 8])
    S.equal = S.sb("equal", [P, 8, 8])
    S.tie = S.sb("tie", [P, 8, 8])
    S.beats = S.sb("beats", [P, 8, 8])
    S.lower = S.sb("lower", [P, 8, 8])
    S.rank = S.sb("rank", [P, 8])
    S.greater_done = S.sig("greater_done")
    S.equal_done = S.sig("equal_done")
    S.tie_done = S.sig("tie_done")
    S.beats_done = S.sig("beats_done")
    S.rank_done = S.sig("rank_done")
    S.lower_set = S.sig("lower_set", per=2)


def make_lower(g, S):
    g.memset(S.lower[:, :, :], 1.0).then_inc(S.lower_set.sem, 1)
    g.wait_ge(S.lower_set.sem, S.lower_set.at(0, 1))
    g.affine_select(out=S.lower[:, :, :], in_=S.lower[:, :, :], compare_op=ALU.is_gt, fill=0.0,
                                   base=0, pattern=[[1, 8], [-1, 8]], channel_multiplier=0).then_inc(S.lower_set.sem, 1)


def relu_experts(nc, K, x_in, x_out, gate_w, gate_b, expert_w, expert_b):
    E = 8
    with ExitStack() as ctx:
        S = Space(nc, ctx, "relu_ffn")
        gate_w_sb = S.sb("gate_w", [P, CH, E])
        gate_b_sb = S.sb("gate_b", [1, E])
        expert_w_sb = S.sb("expert_w", [P, E, CH, DIM])
        expert_b_sb = S.sb("expert_b", [1, E, DIM])
        rank_space(S)
        weight = S.sb("weight", [P, E])
        act_out = S.sb("act_out", [P, E, DIM])
        mixed = S.sb("mixed", [P, DIM])
        y = S.sb("y", [P, DIM])
        turn_ps = S.ps("turn_ps", [P, CH, P])
        logit_ps = S.ps("logit_ps", [P, E])
        out_ps = S.ps("out_ps", [P, 4, 2, DIM])

        N = Norm(S, P, turn_ps[:, :, :])
        weights_loaded = S.dma("weights_loaded", per=4)
        logits_done = S.sig("logits_done")
        score_done = S.sig("score_done")
        weight_done = S.sig("weight_done")
        expert_done = S.sig("expert_done", per=4)
        relu_done = S.sig("relu_done", per=8)
        mixed_done = S.sig("mixed_done")
        y_done = S.sig("y_done", credit=1)
        stored = S.dma("stored", credit=1)

        with nc.Block() as block:
            @block.sync
            def _(sp):
                stored.open(sp)
                sp.dma_start(gate_w_sb[:, :, :], gate_w.rearrange("(c p) e -> p c e", p=P)).then_inc(weights_loaded.sem, 16)
                sp.dma_start(gate_b_sb[:, :], gate_b).then_inc(weights_loaded.sem, 16)
                sp.dma_start(expert_w_sb[:, :, :, :],
                                               expert_w.rearrange("e (c p) o -> p e c o", p=P)).then_inc(weights_loaded.sem, 16)
                sp.dma_start(expert_b_sb[:, :, :], expert_b.rearrange("(a e) o -> a e o", a=1)).then_inc(weights_loaded.sem, 16)
                with sp.Fori(0, TILES) as t:
                    sp.wait_ge(y_done.sem, y_done.before(t))
                    sp.dma_start(N.x[:, :], x_in[t]).then_inc(N.x_loaded.sem, 16)
                    sp.wait_ge(y_done.sem, y_done.at(t))
                    sp.dma_start(x_out[t], y[:, :]).then_inc(stored.sem, 16)
                sp.wait_ge(stored.sem, stored.before(TILES))

            @block.gpsimd
            def _(g):
                make_lower(g, S)

            @block.scalar
            def _(a):
                a.preload_act_table_set("natural_log_exp_and_others")
                a.wait_ge(N.eps_set.sem, N.eps_set.at(0))
                with a.Fori(0, TILES) as t:
                    a.preload_act_table_set("natural_log_exp_and_others")
                    N.scalar(a, t)
                    a.wait_ge(weight_done.sem, weight_done.at(t))
                    for e in range(E):
                        a.wait_ge(expert_done.sem, expert_done.at(t, e // 2 + 1))
                        a.activation(act_out[:, e, :], out_ps[:, e // 2, e % 2, :], ACT.Relu,
                                                  scale=weight[:, e:e + 1]).then_inc(relu_done.sem, 1)

            @block.tensor
            def _(pe):
                pe.wait_ge(weights_loaded.sem, weights_loaded.at(0, 4))
                with pe.Fori(0, TILES) as t:
                    N.tensor(pe, t, K.ident)
                    pe.wait_ge(N.xnT_done.sem, N.xnT_done.at(t))
                    for c in range(CH):
                        pe.matmul(logit_ps[:, :], N.xnT[:, c, :], gate_w_sb[:, c, :], start=(c == 0), stop=False)
                    pe.matmul(logit_ps[:, :], K.ones[0:1, :], gate_b_sb[0:1, :], start=False, stop=True).then_inc(logits_done.sem, 1)
                    for pair in range(E // 2):
                        for c in range(CH):
                            pe.matmul(out_ps[:, pair, :, :], N.xnT[:, c, :], expert_w_sb[:, 2 * pair:2 * pair + 2, c, :],
                                      start=(c == 0), stop=False)
                        pe.matmul(out_ps[:, pair, :, :], K.ones[0:1, :],
                                                 expert_b_sb[0:1, 2 * pair:2 * pair + 2, :], start=False, stop=True).then_inc(expert_done.sem, 1)

            @block.vector
            def _(v):
                N.setup_vector(v)
                y_done.open(v)
                v.wait_ge(S.lower_set.sem, S.lower_set.at(0, 2))
                with v.Fori(0, TILES) as t:
                    N.vector(v, t)
                    v.wait_ge(logits_done.sem, logits_done.at(t))
                    v.tensor_copy(S.score[:, :], logit_ps[:, :]).then_inc(score_done.sem, 1)
                    v.wait_ge(score_done.sem, score_done.at(t))
                    rank_mask_vector(v, t, S)
                    v.tensor_scalar(weight[:, :], S.rank[:, :], 1.5, 0.5, ALU.is_lt, ALU.mult).then_inc(weight_done.sem, 1)
                    v.wait_ge(relu_done.sem, relu_done.at(t, 8))
                    v.tensor_reduce(mixed[:, :], act_out[:, :, :].rearrange("p e d -> p d e"),
                                                  AX.X, ALU.add).then_inc(mixed_done.sem, 1)
                    v.wait_ge(mixed_done.sem, mixed_done.at(t))
                    v.wait_ge(stored.sem, stored.before(t))
                    v.tensor_tensor(y[:, :], mixed[:, :], N.x[:, :], ALU.add).then_inc(y_done.sem, 1)
        S.clear()


def gelu_experts(nc, K, x_in, x_out, gate_w, wd, bd, wu, bu, ws_d, bs_d, ws_u, bs_u):
    E, BOT = 8, 64
    EB = E * BOT
    HID = EB + BOT + E + 1
    CHUNKS = -(-HID // P)
    LAST = HID - (CHUNKS - 1) * P
    with ExitStack() as ctx:
        S = Space(nc, ctx, "gelu_ffn")
        gate_w_sb = S.sb("gate_w", [P, CH, E])
        down_w = S.sb("down_w", [P, CH, EB + BOT])
        down_b = S.sb("down_b", [1, EB + BOT])
        up_w = S.sb("up_w", [P, CHUNKS, DIM])
        rank_space(S)
        peak = S.sb("peak", [P, 1])
        chosen = S.sb("chosen", [P, E])
        total = S.sb("total", [P, 1])
        inv_total = S.sb("inv_total", [P, 1])
        gelu = S.sb("gelu", [P, EB + BOT])
        hidden = S.sb("hidden", [P, HID])
        hiddenT = S.sb("hiddenT", [P, CHUNKS, P])
        y = S.sb("y", [P, DIM])
        turn_ps = S.ps("turn_ps", [P, CH, P])
        logit_ps = S.ps("logit_ps", [P, E])
        down_ps = S.ps("down_ps", [P, 2, 512])
        hidT_ps = S.ps("hidT_ps", [P, 8, P])
        y_ps = S.ps("y_ps", [P, DIM])

        N = Norm(S, P, turn_ps[:, :, :])
        LOADS = 10
        weights_loaded = S.dma("weights_loaded", per=LOADS)
        logits_done = S.sig("logits_done")
        peak_done = S.sig("peak_done")
        score_done = S.sig("score_done")
        chosen_done = S.sig("chosen_done", per=2)
        total_done = S.sig("total_done")
        inv_done = S.sig("inv_done")
        down_done = S.sig("down_done", per=2)
        gelu_done = S.sig("gelu_done", per=2)
        combine_done = S.sig("combine_done")
        hidden_done = S.sig("hidden_done", per=2)
        one_set = S.sig("one_set")
        hidT_done = S.sig("hidT_done")
        hidT_copied = S.sig("hidT_copied", per=2)
        up_done = S.sig("up_done")
        y_done = S.sig("y_done", credit=1)
        stored = S.dma("stored", credit=1)

        with nc.Block() as block:
            @block.sync
            def _(sp):
                stored.open(sp)
                W = weights_loaded
                sp.dma_start(gate_w_sb[:, :, :], gate_w.rearrange("(c p) e -> p c e", p=P)).then_inc(W.sem, 16)
                sp.dma_start(down_w[:, :, 0:EB], wd.rearrange("(c p) n -> p c n", p=P)).then_inc(W.sem, 16)
                sp.dma_start(down_w[:, :, EB:], ws_d.rearrange("(c p) n -> p c n", p=P)).then_inc(W.sem, 16)
                sp.dma_start(down_b[:, 0:EB], bd).then_inc(W.sem, 16)
                sp.dma_start(down_b[:, EB:], bs_d).then_inc(W.sem, 16)
                sp.dma_start(up_w[:, 0:CHUNKS - 1, :], wu.rearrange("(c p) n -> p c n", p=P)).then_inc(W.sem, 16)
                sp.dma_start(up_w[0:BOT, CHUNKS - 1, :], ws_u).then_inc(W.sem, 16)
                sp.dma_start(up_w[BOT:BOT + E, CHUNKS - 1, :], bu).then_inc(W.sem, 16)
                sp.dma_start(up_w[BOT + E:LAST, CHUNKS - 1, :], bs_u).then_inc(W.sem, 16)
                with sp.Fori(0, TILES) as t:
                    sp.wait_ge(y_done.sem, y_done.before(t))
                    sp.dma_start(N.x[:, :], x_in[t]).then_inc(N.x_loaded.sem, 16)
                    sp.wait_ge(y_done.sem, y_done.at(t))
                    sp.dma_start(x_out[t], y[:, :]).then_inc(stored.sem, 16)
                sp.wait_ge(stored.sem, stored.before(TILES))

            @block.gpsimd
            def _(g):
                make_lower(g, S)
                g.memset(hidden[:, HID - 1:HID], 1.0).then_inc(one_set.sem, 1)

            @block.scalar
            def _(a):
                a.preload_act_table_set("natural_log_exp_and_others")
                a.wait_ge(N.eps_set.sem, N.eps_set.at(0))
                with a.Fori(0, TILES) as t:
                    a.preload_act_table_set("natural_log_exp_and_others")
                    N.scalar(a, t)
                    a.wait_ge(peak_done.sem, peak_done.at(t))
                    a.activation(S.score[:, :], logit_ps[:, :], ACT.Exp, bias=peak[:, 0:1]).then_inc(score_done.sem, 1)
                    for n, (lo, hi) in enumerate(((0, EB), (EB, EB + BOT))):
                        a.wait_ge(down_done.sem, down_done.at(t, n + 1))
                        a.activation(gelu[:, lo:hi], down_ps[:, n, 0:hi - lo], ACT.Gelu).then_inc(gelu_done.sem, 1)
                    a.wait_ge(hidT_done.sem, hidT_done.at(t))
                    a.copy(hiddenT[:, 0:CHUNKS - 1, :], hidT_ps[:, 0:CHUNKS - 1, :]).then_inc(hidT_copied.sem, 1)
                    a.copy(hiddenT[0:LAST, CHUNKS - 1, :], hidT_ps[0:LAST, CHUNKS - 1, :]).then_inc(hidT_copied.sem, 1)

            @block.tensor
            def _(pe):
                pe.wait_ge(weights_loaded.sem, weights_loaded.at(0, 9))
                pe.wait_ge(one_set.sem, one_set.at(0))
                with pe.Fori(0, TILES) as t:
                    N.tensor(pe, t, K.ident)
                    pe.wait_ge(N.xnT_done.sem, N.xnT_done.at(t))
                    for c in range(CH):
                        mm = pe.matmul(logit_ps[:, :], N.xnT[:, c, :], gate_w_sb[:, c, :], start=(c == 0), stop=(c == 1))
                    mm.then_inc(logits_done.sem, 1)
                    for n, (lo, hi) in enumerate(((0, EB), (EB, EB + BOT))):
                        for c in range(CH):
                            pe.matmul(down_ps[:, n, 0:hi - lo], N.xnT[:, c, :], down_w[:, c, lo:hi],
                                      start=(c == 0), stop=False)
                        pe.matmul(down_ps[:, n, 0:hi - lo], K.ones[0:1, :], down_b[0:1, lo:hi],
                                               start=False, stop=True).then_inc(down_done.sem, 1)
                    pe.wait_ge(hidden_done.sem, hidden_done.at(t, 2))
                    pe.wait_ge(combine_done.sem, combine_done.at(t))
                    for c in range(CHUNKS):
                        w = P if c < CHUNKS - 1 else LAST
                        turn = pe.transpose(hidT_ps[0:w, c, :], hidden[:, c * P:c * P + w], K.ident[:, :])
                    turn.then_inc(hidT_done.sem, 1)
                    pe.wait_ge(hidT_copied.sem, hidT_copied.at(t, 2))
                    for c in range(CHUNKS):
                        w = P if c < CHUNKS - 1 else LAST
                        mm = pe.matmul(y_ps[:, :], hiddenT[0:w, c, :], up_w[0:w, c, :],
                                       start=(c == 0), stop=(c == CHUNKS - 1))
                    mm.then_inc(up_done.sem, 1)

            @block.vector
            def _(v):
                N.setup_vector(v)
                y_done.open(v)
                v.wait_ge(S.lower_set.sem, S.lower_set.at(0, 2))
                with v.Fori(0, TILES) as t:
                    N.vector(v, t)
                    v.wait_ge(logits_done.sem, logits_done.at(t))
                    v.tensor_reduce(peak[:, :], logit_ps[:, :], AX.X, ALU.max, negate=True).then_inc(peak_done.sem, 1)
                    v.wait_ge(score_done.sem, score_done.at(t))
                    rank_mask_vector(v, t, S)
                    v.tensor_scalar(chosen[:, :], S.rank[:, :], 1.5, None, ALU.is_lt).then_inc(chosen_done.sem, 1)
                    v.wait_ge(chosen_done.sem, chosen_done.at(t, 1))
                    v.tensor_tensor(chosen[:, :], chosen[:, :], S.score[:, :], ALU.mult).then_inc(chosen_done.sem, 1)
                    v.wait_ge(chosen_done.sem, chosen_done.at(t, 2))
                    v.tensor_reduce(total[:, :], chosen[:, :], AX.X, ALU.add).then_inc(total_done.sem, 1)
                    v.wait_ge(total_done.sem, total_done.at(t))
                    v.reciprocal(inv_total[:, :], total[:, :]).then_inc(inv_done.sem, 1)
                    v.wait_ge(inv_done.sem, inv_done.at(t))
                    combine = hidden[:, EB + BOT:EB + BOT + E]
                    v.tensor_scalar(combine, chosen[:, :], inv_total[:, 0:1], None, ALU.mult).then_inc(combine_done.sem, 1)
                    v.wait_ge(gelu_done.sem, gelu_done.at(t, 2))
                    v.wait_ge(combine_done.sem, combine_done.at(t))
                    v.tensor_tensor(
                        hidden[:, 0:EB].rearrange("p (e b) -> p e b", e=E), gelu[:, 0:EB].rearrange("p (e b) -> p e b", e=E),
                        combine.unsqueeze(2).broadcast_to([P, E, BOT]), ALU.mult).then_inc(hidden_done.sem, 1)
                    v.tensor_copy(hidden[:, EB:EB + BOT], gelu[:, EB:EB + BOT]).then_inc(hidden_done.sem, 1)
                    v.wait_ge(up_done.sem, up_done.at(t))
                    v.wait_ge(stored.sem, stored.before(t))
                    v.tensor_tensor(y[:, :], y_ps[:, :], N.x[:, :], ALU.add).then_inc(y_done.sem, 1)
        S.clear()




class Constants:
    pass


def program(nc, A, out):
    K = Constants()
    phases = [0, 1, 2, 3, 4, 5]
    with ExitStack() as ctx:
        S = Space(nc, ctx, "const")
        K.ident = S.sb("ident", [P, P])
        K.ones = S.sb("ones", [P, P])
        ident_done = S.sig("ident_done", per=2)
        ones_done = S.sig("ones_done")
        with nc.Block() as block:
            @block.gpsimd
            def _(g):
                make_identity(g, K.ident, ident_done, 0)
                g.memset(K.ones[:, :], 1.0).then_inc(ones_done.sem, 1)

        steps = [
            lambda x, y: context_attention(nc, K, x, y, A),
            lambda x, y: gated_attention(nc, K, x, y, A),
            lambda x, y: relu_experts(nc, K, x, y, A["L0_ffn_gate_w"], A["L0_ffn_gate_b"], A["L0_ffn_expert_w"], A["L0_ffn_expert_b"]),
            lambda x, y: context_gqa(nc, K, x, y, A),
            lambda x, y: rotary_attention(nc, K, x, y, A),
            lambda x, y: gelu_experts(nc, K, x, y, A["L1_ffn_gate_w"], A["L1_ffn_wd"], A["L1_ffn_bd"], A["L1_ffn_wu"],
                                      A["L1_ffn_bu"], A["L1_ffn_ws_d"], A["L1_ffn_bs_d"], A["L1_ffn_ws_u"], A["L1_ffn_bs_u"]),
        ]
        by_batch = {0: True, 3: True}

        def view(dram, phase):
            if phase in by_batch:
                return dram
            return dram.rearrange("(t b) s d -> t (b s) d", t=TILES)

        dram = A["x"]
        for n, phase in enumerate(phases):
            last = n == len(phases) - 1
            target = out if last else nc.dram_tensor(f"x_after_{phase}", [BATCH, SEQ, DIM], F32, kind="Internal").ap()
            steps[phase](view(dram, phase), view(target, phase))
            dram = target


def _inputs(inputs):
    def row(name):
        return inputs[name].reshape(1, -1)

    def cols(name):
        return inputs[name].reshape(-1, 128).T

    A = {"x": inputs["x"]}
    A["L0_ffn_gate_w"] = inputs["L0_ffn_gate_w"]
    A["L0_ffn_gate_b"] = row("L0_ffn_gate_b")
    A["L0_ffn_expert_w"] = inputs["L0_ffn_expert_w"]
    A["L0_ffn_expert_b"] = inputs["L0_ffn_expert_b"]
    A["L1_ffn_gate_w"] = inputs["L1_ffn_gate_w"].T
    A["L1_ffn_wd"] = inputs["L1_ffn_wd"].reshape(512, 256).T
    A["L1_ffn_bd"] = row("L1_ffn_bd")
    A["L1_ffn_wu"] = inputs["L1_ffn_wu"].transpose(0, 2, 1).reshape(512, 256)
    A["L1_ffn_bu"] = inputs["L1_ffn_bu"]
    A["L1_ffn_ws_d"] = inputs["L1_ffn_ws_d"].T
    A["L1_ffn_bs_d"] = row("L1_ffn_bs_d")
    A["L1_ffn_ws_u"] = inputs["L1_ffn_ws_u"].T
    A["L1_ffn_bs_u"] = row("L1_ffn_bs_u")

    A["ctxT"] = inputs["ctx_2048"].transpose(0, 2, 1)
    A["lens"] = inputs["_lenS2"].reshape(BATCH, 1, 1)
    for name in ("w_q", "w_k", "w_v", "w_k_img", "w_v_img", "w_o"):
        A[f"L0_xattn_{name}"] = inputs[f"L0_xattn_{name}"].T
    for name in ("b_q", "b_o"):
        A[f"L0_xattn_{name}"] = row(f"L0_xattn_{name}")
    for name in ("b_k", "b_v", "b_k_img", "b_v_img", "g_q", "g_k", "g_k_img"):
        A[f"L0_xattn_{name}"] = cols(f"L0_xattn_{name}")
    A["pos"] = inputs["pos_BxS2"].reshape(BATCH, 1, CTX)
    A["draft_pos"] = inputs["itok_BxS_4096_4607"].reshape(BATCH, 1, SEQ)
    for name in ("Wq", "Wk", "Wv", "Wo"):
        A[f"L1_xattn_{name}"] = inputs[f"L1_xattn_{name}"].T
    for name in ("q_norm_w", "k_norm_w"):
        A[f"L1_xattn_{name}"] = cols(f"L1_xattn_{name}")
    w = inputs["L0_attn_w_qkv"]
    H, KV, D = 16, 4, 128
    wq = w[0:H * D].reshape(2, 2, 4, D // 2, 2, DIM).transpose(0, 2, 4, 1, 3, 5).reshape(H * D, DIM)
    wk = w[2 * H * D:2 * H * D + KV * D].reshape(2, 2, D // 2, 2, DIM).transpose(0, 3, 1, 2, 4).reshape(KV * D, DIM)
    A["L0_attn_wqk"] = np.concatenate([wq, wk], axis=0).T
    A["L0_attn_wg"] = w[H * D:2 * H * D].T
    A["L0_attn_wv"] = w[2 * H * D + KV * D:].T
    A["L0_attn_w_o"] = inputs["L0_attn_w_o"].T
    for name in ("q_norm_w", "q_norm_b", "k_norm_w", "k_norm_b"):
        A[f"L0_attn_{name}"] = inputs[f"L0_attn_{name}"].reshape(D // 2, 2)
    for name in ("qn_g", "qn_b", "kvn_g", "kvn_b"):
        A[f"L1_attn_{name}"] = cols(f"L1_attn_{name}")
    for name in ("bq", "bkv", "bo", "ln_g", "ln_b"):
        A[f"L1_attn_{name}"] = row(f"L1_attn_{name}")
    for name in ("Wq", "Wkv", "Wo"):
        A[f"L1_attn_{name}"] = inputs[f"L1_attn_{name}"]
    return A


def _tables():
    f = np.float32
    pos = np.arange(SEQ, dtype=f)
    inverse = (f(1.0) / f(1e6) ** (np.arange(0, 128, 2, dtype=f) / f(128))).astype(f)
    gated = np.outer(inverse, pos).astype(f)
    gated = np.concatenate([gated, gated], axis=1)
    freqs = (np.arange(0, 16, 2, dtype=f) / f(16) * np.log(f(30000.0))).astype(f)
    rotary = (pos[:, None] * freqs[None, :]).astype(f)
    rotary = np.concatenate([rotary, rotary], axis=0)
    gqa = (f(1.0) / f(10000.0) ** (np.arange(0, 128, 2, dtype=f) / f(128))).astype(f)
    sign = np.repeat(np.array([1.0, -1.0], f), 64).reshape(128, 1)
    return {"gqa_inv_freq": np.concatenate([gqa, gqa]).reshape(128, 1), "gqa_sign": sign,
            "gated_cos": np.cos(gated), "gated_sin": np.sin(gated),
            "rotary_cos": np.cos(rotary), "rotary_sin": np.sin(rotary)}


def kernel(**inputs):
    import concourse.bacc as _bacc
    from concourse.bass_utils import run_bass_kernel_spmd as _run

    nc = _bacc.Bacc("TRN2", target_bir_lowering=False, num_devices=1)
    arrays, A = {}, {}
    laid_out = _inputs({k: np.asarray(v) for k, v in inputs.items()})
    laid_out.update(_tables())
    for name, a in laid_out.items():
        a = np.ascontiguousarray(a)
        arrays[f"in_{name}"] = a
        A[name] = nc.dram_tensor(f"in_{name}", a.shape, mybir.dt.from_np(a.dtype), kind="ExternalInput").ap()
    out = nc.dram_tensor("out_x", [BATCH, SEQ, DIM], F32, kind="ExternalOutput").ap()
    program(nc, A, out)
    r = _run(nc, [arrays], core_ids=[0])
    return r.results[0]["out_x"]
```
